# Optimizing a Trainium2 kernel written in Bass

```python
import numpy as np
import jax
import jax.numpy as jnp

def _softmax(x, axis=-1):
    return jax.nn.softmax(x, axis=axis)

def _gelu(x):
    return jax.nn.gelu(x, approximate=True)

def _silu(x):
    return jax.nn.silu(x)

def _sigmoid(x):
    return jax.nn.sigmoid(x)

def _layernorm(x, axis=-1, eps=1e-05):
    m = jnp.mean(x, axis=axis, keepdims=True)
    v = jnp.var(x, axis=axis, keepdims=True)
    return (x - m) / jnp.sqrt(v + eps)

def _scatter_add(tgt, idx, src, axis=0):
    return tgt.at[idx].add(src)

def _segment_sum(src, seg, n):
    return jax.ops.segment_sum(src, seg, n)
kernel_name = 'mk_gnn_ffn_d1_gnn_r8_d2da37'

def setup_inputs(seed: int=0):
    np.random.seed(seed)
    _w = jnp.asarray

    def _rec_inputs():
        import jax
        import jax.numpy as jnp
        _gk = jax.random.key(seed)
        x = -0.0003713 + 1 * jax.random.normal(jax.random.fold_in(_gk, 1), (6250, 256), jnp.float32)
        src = jax.random.randint(jax.random.fold_in(_gk, 2), (200000,), 0, 6250, jnp.int32)
        dst = jnp.minimum((6250 * jax.random.uniform(jax.random.fold_in(_gk, 3), (200000,)) ** 2.0).astype(jnp.int32), 49999)
        _o = jnp.argsort(dst, stable=True)
        src = src[_o]
        dst = dst[_o]
        return (x, src, dst)
    x, src, dst = _rec_inputs()

    def _L0_gnn_setup():
        import jax, jax.numpy as jnp
        import numpy as np
        N_NODES = 6250

        def _gcn_norm(edge_index, num_nodes):
            src, dst = (edge_index[0], edge_index[1])
            loop = jnp.arange(num_nodes, dtype=src.dtype)
            src = jnp.concatenate([src, loop])
            dst = jnp.concatenate([dst, loop])
            deg = jax.ops.segment_sum(jnp.ones_like(dst, dtype=jnp.float32), dst, num_segments=num_nodes)
            dinv = jax.lax.rsqrt(deg)
            norm = dinv[src] * dinv[dst]
            return (src, dst, norm)

        def _gcn_conv(x, W, b, src, dst, norm, num_nodes):
            h = x @ W
            msg = h[src] * norm[:, None]
            agg = jax.ops.segment_sum(msg, dst, num_segments=num_nodes)
            return agg + b
        key = jax.random.key(seed)
        ks = jax.random.split(key, 8)
        in_dim, hidden_dim, out_dim = (256, 256, 256)
        x = jax.random.normal(ks[0], (N_NODES, in_dim), dtype=jnp.float32)
        edge_index = jax.random.randint(ks[1], (2, 200000), 0, N_NODES, dtype=jnp.int32)

        def glorot(k, fan_in, fan_out):
            s = jnp.sqrt(6.0 / (fan_in + fan_out)).astype(jnp.float32)
            return jax.random.uniform(k, (fan_in, fan_out), jnp.float32, -s, s)
        return {'x': x, 'W1': glorot(ks[2], in_dim, hidden_dim), 'b1': jnp.zeros((hidden_dim,), jnp.float32), 'W2': glorot(ks[3], hidden_dim, hidden_dim), 'b2': jnp.zeros((hidden_dim,), jnp.float32), 'W3': glorot(ks[4], hidden_dim, out_dim), 'b3': jnp.zeros((out_dim,), jnp.float32), 'edge_index': edge_index}
    _L0_gnn_all = _L0_gnn_setup()
    _L0_gnn_in = {k: v for k, v in _L0_gnn_all.items() if k in ('W1', 'b1', 'W2', 'b2', 'W3', 'b3')}
    del _L0_gnn_all

    def _L0_ffn_setup():
        import jax, jax.numpy as jnp
        import numpy as np
        B, S, D = (8, 512, 256)
        H = 4 * D
        CAPACITY = 0.5
        key = jax.random.key(seed)
        ks = jax.random.split(key, 6)
        x = jax.random.normal(ks[0], (B, S, D), dtype=jnp.float32)
        attention_mask = jnp.zeros((B, 1, 1, S), dtype=jnp.float32)
        wr = jax.random.normal(ks[1], (D, 1), dtype=jnp.float32) * 0.02
        br = jnp.zeros((1,), dtype=jnp.float32)
        w1 = jax.random.normal(ks[2], (D, H), dtype=jnp.float32) * 0.02
        b1 = jnp.zeros((H,), dtype=jnp.float32)
        w2 = jax.random.normal(ks[3], (H, D), dtype=jnp.float32) * 0.02
        b2 = jnp.zeros((D,), dtype=jnp.float32)
        return {'x': x, 'attention_mask': attention_mask, 'wr': wr, 'br': br, 'w1': w1, 'b1': b1, 'w2': w2, 'b2': b2}
    _L0_ffn_all = _L0_ffn_setup()
    _L0_ffn_in = {k: v for k, v in _L0_ffn_all.items() if k in ('attention_mask', 'wr', 'br', 'w1', 'b1', 'w2', 'b2')}
    del _L0_ffn_all
    return {'x': x, 'src': src, 'dst': dst, 'L0_gnn_W1': _L0_gnn_in['W1'], 'L0_gnn_b1': _L0_gnn_in['b1'], 'L0_gnn_W2': _L0_gnn_in['W2'], 'L0_gnn_b2': _L0_gnn_in['b2'], 'L0_gnn_W3': _L0_gnn_in['W3'], 'L0_gnn_b3': _L0_gnn_in['b3'], 'L0_ffn_attention_mask': _L0_ffn_in['attention_mask'], 'L0_ffn_wr': _L0_ffn_in['wr'], 'L0_ffn_br': _L0_ffn_in['br'], 'L0_ffn_w1': _L0_ffn_in['w1'], 'L0_ffn_b1': _L0_ffn_in['b1'], 'L0_ffn_w2': _L0_ffn_in['w2'], 'L0_ffn_b2': _L0_ffn_in['b2']}

def reference(x, src, dst, L0_gnn_W1, L0_gnn_b1, L0_gnn_W2, L0_gnn_b2, L0_gnn_W3, L0_gnn_b3, L0_ffn_attention_mask, L0_ffn_wr, L0_ffn_br, L0_ffn_w1, L0_ffn_b1, L0_ffn_w2, L0_ffn_b2):
    import jax
    import jax.numpy as jnp

    def _L0_gnn_ref(x, W1, b1, W2, b2, W3, b3, edge_index):
        import jax, jax.numpy as jnp
        import numpy as np
        N_NODES = 6250

        def _gcn_norm(edge_index, num_nodes):
            src, dst = (edge_index[0], edge_index[1])
            loop = jnp.arange(num_nodes, dtype=src.dtype)
            src = jnp.concatenate([src, loop])
            dst = jnp.concatenate([dst, loop])
            deg = jax.ops.segment_sum(jnp.ones_like(dst, dtype=jnp.float32), dst, num_segments=num_nodes)
            dinv = jax.lax.rsqrt(deg)
            norm = dinv[src] * dinv[dst]
            return (src, dst, norm)

        def _gcn_conv(x, W, b, src, dst, norm, num_nodes):
            h = x @ W
            msg = h[src] * norm[:, None]
            agg = jax.ops.segment_sum(msg, dst, num_segments=num_nodes)
            return agg + b
        num_nodes = x.shape[0]
        src, dst, norm = _gcn_norm(edge_index, num_nodes)
        h = jax.nn.relu(_gcn_conv(x, W1, b1, src, dst, norm, num_nodes))
        h = jax.nn.relu(_gcn_conv(h, W2, b2, src, dst, norm, num_nodes))
        return _gcn_conv(h, W3, b3, src, dst, norm, num_nodes)

    def _L0_ffn_ref(x, attention_mask, wr, br, w1, b1, w2, b2):
        import jax, jax.numpy as jnp
        import numpy as np
        B, S, D = (8, 512, 256)
        H = 4 * D
        CAPACITY = 0.5
        b, s, d = x.shape
        weights = (jnp.einsum('bsd,do->bso', x, wr) + br)[..., 0]
        k = max(1, int(CAPACITY * s))
        kk = k - 1 if k > 1 else 1
        _, idx = jax.lax.top_k(weights, k)
        sel_idx = idx[:, :kk]
        sel = jnp.take_along_axis(x, sel_idx[:, :, None], axis=1)
        h = jax.nn.gelu(jnp.einsum('bkd,dh->bkh', sel, w1) + b1)
        y = jnp.einsum('bkh,hd->bkd', h, w2) + b2
        w_sel = jnp.take_along_axis(weights, sel_idx, axis=1)
        y = y * w_sel[..., None]
        batch_idx = jnp.arange(b)[:, None]
        processed = jnp.zeros_like(x).at[batch_idx, sel_idx].set(y)
        return processed + x
    edge_index = jnp.stack([src, dst])
    x = x + _L0_gnn_ref(_layernorm(x, axis=-1), L0_gnn_W1, L0_gnn_b1, L0_gnn_W2, L0_gnn_b2, L0_gnn_W3, L0_gnn_b3, edge_index)
    x = x + _L0_ffn_ref(_layernorm(x, axis=-1)[None], L0_ffn_attention_mask, L0_ffn_wr, L0_ffn_br, L0_ffn_w1, L0_ffn_b1, L0_ffn_w2, L0_ffn_b2)[0]
    return x

_drawn_inputs = setup_inputs


def setup_inputs(seed=0):
    import zlib

    import numpy as np

    out = dict(_drawn_inputs(seed))
    spreads = {'L0_gnn_b1': (0.0, 0.288),
     'L0_gnn_b2': (0.0, 0.1),
     'L0_gnn_b3': (0.0, 0.1),
     'L0_ffn_b1': (0.0, 0.8),
     'L0_ffn_b2': (0.0, 0.733)}
    factors = {'L0_gnn_W1': 7.881, 'L0_ffn_wr': 3.912, 'L0_ffn_w1': 4.614, 'L0_ffn_w2': 4.286}
    for name, (base, spread) in spreads.items():
        noise = np.random.default_rng([zlib.crc32(name.encode()), seed]).standard_normal(out[name].shape)
        drawn = base * np.exp(spread * noise) if base else spread * noise
        out[name] = jnp.asarray(drawn.astype(out[name].dtype))
    for name, factor in factors.items():
        out[name] = (out[name] * factor).astype(out[name].dtype)
    return out
```

```python
from contextlib import ExitStack

import numpy as np
import concourse.bass as bass
from concourse import mybir

ALU = mybir.AluOpType
ACT = mybir.ActivationFunctionType
AX = mybir.AxisListType
F32 = mybir.dt.float32
F16 = mybir.dt.float16
I32 = mybir.dt.int32
RED = bass.bass_isa.ReduceOp

P = 128
D = 256
HALVES = D // P
N = 6250
TILES = -(-N // P)
NP = TILES * P
LAST = N - (TILES - 1) * P
E = 200000
EJ = 13
ET = P * EJ
EFULL = E // (EJ * P)
EREST = E - EFULL * EJ * P
W = 16
HW = W // 2
WB = HW * TILES
WC = 2 * WB
WINDOWS = NP // W
WP = 98
WG = WINDOWS // WP
BLK = 448
BLOCKS = NP // BLK
PAIRS = BLOCKS // 2
BW = BLK // W
LW = 4
RING = 8
KC = 7
CHUNKS = TILES // KC
PAD = 8191
HID = 4 * D
HM = HID // P
KEEP = max(1, int(0.5 * N)) - 1
ASCALE = 0.25
EPS = 1e-5
BN = 6


def build(nc, x, src, dst, gw, gb, wr, br, w1, b1, w2, b2, out):
    ctx = ExitStack()
    with ctx:
        def sb(name, shape, dt):
            return ctx.enter_context(nc.sbuf_tensor(name, shape, dt))

        def sem(name):
            return ctx.enter_context(nc.semaphore(name))

        adj = nc.dram_tensor("adj", (BLOCKS, P, TILES * BLK), F16, kind="Internal").ap()
        tile_ends = nc.dram_tensor("tile_ends", (2, ET), F32, kind="Internal").ap()
        route_row = nc.dram_tensor("route_row", (TILES, P), F32, kind="Internal").ap()

        big_a = sb("big_a", [P, TILES * D], F32)
        big_b = sb("big_b", [P, TILES * BLK], F16)
        feat = sb("feat", [P, HALVES, NP], F32)
        dinv_row = sb("dinv_row", [P, NP], F32)
        dinv_col = sb("dinv_col", [P, TILES], F32)
        ident = sb("ident", [P, P], F32)
        ones = sb("ones", [P, P], F32)
        ones16 = sb("ones16", [P, P], F16)
        stage = sb("stage", [P, 2, D], F32)
        gw_sb = sb("gw_sb", [P, 3, HALVES, D], F32)
        gb_sb = sb("gb_sb", [P, 3, HALVES], F32)
        small = sb("small", [P, 64], F32)
        smalli = sb("smalli", [P, 8], I32)
        mean = sb("mean", [P, TILES], F32)
        rstd = sb("rstd", [P, TILES], F32)
        hh = big_a[:].bitcast(F16).rearrange("p (q f n) -> p q f n", q=2, f=HALVES)
        blocks16 = [big_a[:].bitcast(F16)[:, 0:TILES * BLK].rearrange("p (s d) -> p s d", s=TILES),
                    big_b[:].rearrange("p (s d) -> p s d", s=TILES)]
        chunk = big_b[:].rearrange("p (c k d) -> p c k d", c=CHUNKS, k=KC)
        nodes = big_a[:].rearrange("p (t d) -> p t d", t=TILES)

        c_init = sem("c_init")

        with nc.Block() as block:
            @block.gpsimd
            def _(pool):
                pool.memset(ident[:], 0.0).then_inc(c_init, 1)
                pool.wait_ge(c_init, 1)
                pool.affine_select(out=ident[:], in_=ident[:], compare_op=ALU.not_equal, fill=1.0, base=0,
                                   pattern=[[-1, P]], channel_multiplier=1).then_inc(c_init, 1)

            @block.vector
            def _(dve):
                dve.memset(ones[:], 1.0)
                dve.memset(ones16[:], 1.0)

            @block.sync
            def _(sp):
                s = sem("s_weights")
                for l in range(3):
                    sp.dma_start(gw_sb[:, l], gw[l].rearrange("(k p) n -> p k n", p=P)).then_inc(s, 16)
                    with nc.allow_non_contiguous_dma(reason="a bias of 256 values"):
                        sp.dma_start(gb_sb[:, l], gb[l].rearrange("(k p) -> p k", p=P)).then_inc(s, 16)
                sp.wait_ge(s, 96)

        build_adjacency(nc, sem, src, dst, adj, tile_ends, big_a, big_b, dinv_row, dinv_col, feat, ident, ones16, blocks16)
        load_and_norm(nc, sem, x, nodes, feat, ident, mean, rstd, stage)
        for l in range(3):
            layer(nc, sem, l, adj, feat, hh, chunk, dinv_row, dinv_col, gw_sb, gb_sb, small, smalli, stage)
        finish(nc, sem, x, nodes, feat, big_b, dinv_row, ident, ones, mean, rstd, stage, small, route_row,
               wr, br, w1, b1, w2, b2, out)


def build_adjacency(nc, sem, src, dst, adj, tile_ends, big_a, big_b, dinv_row, dinv_col, feat, ident, ones16, blocks16):
    with ExitStack() as ctx:
        def sb(name, shape, dt):
            return ctx.enter_context(nc.sbuf_tensor(name, shape, dt))

        def ps(name, shape, dt):
            return ctx.enter_context(nc.psum_tensor(name, shape, dt))

        tmp = feat[:].rearrange("p f n -> p (f n)")
        dst_i = tmp[:, 0:ET].bitcast(I32)
        src_i = tmp[:, ET:2 * ET].bitcast(I32)
        dst_f = tmp[:, 2 * ET:3 * ET]
        key_r = tmp[:, 3 * ET:4 * ET]
        slo_r = tmp[:, 4 * ET:5 * ET]
        low_b = tmp[:, 5 * ET:6 * ET]
        high_b = tmp[:, 6 * ET:7 * ET]
        iota_i = dinv_row[:, 0:ET].bitcast(I32)
        up = dinv_row[:, ET:2 * ET]
        down = dinv_row[:, 2 * ET:3 * ET]
        key_t = tmp[:, 0:ET]
        slo_t = tmp[:, ET:2 * ET]
        ohi = tmp[:, 2 * ET:2 * ET + RING * WC // 2].bitcast(F16)
        olo = tmp[:, 2 * ET + RING * WC // 2:2 * ET + RING * (WC + P) // 2].bitcast(F16)
        scratch = big_a[:, 0:ET]
        iota16 = sb("iota16", [P, WC], F16)
        base = sb("base", [P, WINDOWS], F32)
        base_i = sb("base_i", [P, WINDOWS], I32)
        thr = sb("thr", [WP, 2, WG], F32)
        thr_i = sb("thr_i", [WP, 2, WG], I32)
        ends = sb("ends", [P, 2, EJ], F32)
        found = sb("found", [WP, 2, WG], F32)
        table = sb("table", [WP, WG, 2], I32)
        ranges = sb("ranges", [1, 2 * WINDOWS], I32)
        zeros16 = sb("zeros16", [P, BLK], F16)
        place = sb("place", [P, 2 * P - W], F16)
        spread = sb("spread", [P, 2, TILES + WB], F16)
        e_pad, e_rows, e_dve, e_pool, e_ends, e_rt, e_tr = (sem(n) for n in (
            "e_pad", "e_rows", "e_dve", "e_pool", "e_ends", "e_roundtrip", "e_transposed"))
        e_bc, e_table, e_tload = sem("e_bc"), sem("e_table"), sem("e_tload")

        with ExitStack() as c2:
            tp = [c2.enter_context(nc.psum_tensor(f"tp{i}", [P, 4, P], F32)) for i in range(8)]
            with nc.Block() as block:
                @block.gpsimd
                def _(pool):
                    pool.iota(iota_i, pattern=[[1, ET]], base=0, channel_multiplier=0).then_inc(e_pool, 1)
                    pool.iota(base_i[:], pattern=[[1, WINDOWS]], base=0, channel_multiplier=0).then_inc(e_pool, 1)
                    pool.iota(thr_i[:, 0, :], pattern=[[W, WG]], base=0, channel_multiplier=W * WG).then_inc(e_pool, 1)
                    pool.iota(thr_i[:, 1, :], pattern=[[W, WG]], base=W, channel_multiplier=W * WG).then_inc(e_pool, 1)
                    pool.memset(place[:], 0.0).then_inc(e_pool, 1)
                    pool.memset(spread[:], 0.0).then_inc(e_pool, 1)
                    pool.memset(zeros16[:], 0.0).then_inc(e_pool, 1)
                    pool.wait_ge(e_pool, 7)
                    pool.affine_select(out=place[0:W], in_=place[0:W], compare_op=ALU.not_equal, fill=1.0,
                                       base=P - W, pattern=[[-1, 2 * P - W]], channel_multiplier=1).then_inc(e_pool, 1)
                    for h in range(2):
                        pool.affine_select(out=spread[0:W, h], in_=spread[0:W, h], compare_op=ALU.not_equal, fill=1.0,
                                           base=TILES - HW * h * TILES, pattern=[[-1, TILES + WB]],
                                           channel_multiplier=TILES).then_inc(e_pool, 1)

                @block.sync
                def _(sp):
                    sp.wait_ge(e_pad, 2)
                    rows = lambda a: a[0:EFULL * EJ * P].rearrange("(p e) -> p e", p=EFULL)
                    rest = lambda a: a[EFULL * EJ * P:E].rearrange("(p e) -> p e", p=1)
                    sp.dma_start(dst_i[0:EFULL, :], rows(dst)).then_inc(e_rows, 16)
                    sp.dma_start(dst_i[EFULL:EFULL + 1, 0:EREST], rest(dst)).then_inc(e_rows, 16)
                    sp.dma_start(src_i[0:EFULL, :], rows(src)).then_inc(e_rows, 16)
                    sp.dma_start(src_i[EFULL:EFULL + 1, 0:EREST], rest(src)).then_inc(e_rows, 16)
                    sp.wait_ge(e_ends, 2)
                    sp.dma_start(tile_ends.rearrange("a (p j) -> p a j", p=P), ends[:]).then_inc(e_rt, 16)
                    sp.wait_ge(e_rt, 16)
                    sp.dma_start(low_b, tile_ends[0:1, :].broadcast_to([P, ET])).then_inc(e_bc, 16)
                    sp.dma_start(high_b, tile_ends[1:2, :].broadcast_to([P, ET])).then_inc(e_bc, 16)
                    sp.wait_ge(e_table, 1)
                    sp.dma_start(ranges[0:1, :], table[:].rearrange("p g c -> p (g c)")).then_inc(e_tload, 16)
                    sp.wait_ge(e_tload, 16)

                @block.vector
                def _(dve):
                    n = [0]

                    def done(ins):
                        n[0] += 1
                        ins.then_inc(e_dve, 1)
                        dve.wait_ge(e_dve, n[0])

                    dve.memset(dst_i, PAD).then_inc(e_pad, 1)
                    dve.memset(src_i, 0).then_inc(e_pad, 1)
                    dve.wait_ge(e_pool, 4)
                    done(dve.tensor_copy(iota16[:], iota_i[:, 0:WC]))
                    done(dve.tensor_scalar(base[:], base_i[:], float(-W * TILES), None, ALU.mult))
                    done(dve.tensor_scalar(up, iota_i, 1.0, None, ALU.add))
                    done(dve.tensor_scalar(down, iota_i, -1.0, float(ET), ALU.mult, ALU.add))
                    done(dve.tensor_copy(thr[:], thr_i[:]))
                    dve.wait_ge(e_rows, 64)
                    done(dve.tensor_copy(dst_f, dst_i))
                    rows3 = dst_f.rearrange("p (j e) -> p j e", j=EJ)
                    dve.tensor_reduce(ends[:, 0, :], rows3, AX.X, ALU.min).then_inc(e_ends, 1)
                    dve.tensor_reduce(ends[:, 1, :], rows3, AX.X, ALU.max).then_inc(e_ends, 1)
                    done(dve.tensor_scalar(slo_r.bitcast(I32), src_i, 7, None, ALU.arith_shift_right))
                    done(dve.scalar_tensor_tensor(key_r, dst_f, float(TILES), slo_r.bitcast(I32), ALU.mult, ALU.add))
                    done(dve.tensor_scalar(dst_i, src_i, P - 1, None, ALU.bitwise_and))
                    done(dve.tensor_copy(slo_r, dst_i))
                    for g in range(8):
                        dve.wait_ge(e_tr, g + 1)
                        r, j0, k = g // 4, 4 * (g % 4), min(4, EJ - 4 * (g % 4))
                        t = (key_t, slo_t)[r].rearrange("p (q j) -> p j q", j=EJ)
                        done(dve.tensor_copy(t[:, j0:j0 + k, :], tp[g][:, 0:k, :]))
                    dve.wait_ge(e_bc, 32)
                    for g in range(WG):
                        done(dve.scalar_tensor_tensor(scratch[0:WP], high_b[0:WP], thr[:, 0, g:g + 1], down[0:WP],
                                                      ALU.is_ge, ALU.mult))
                        done(dve.tensor_reduce(found[:, 0, g:g + 1], scratch[0:WP], AX.X, ALU.max))
                        done(dve.scalar_tensor_tensor(scratch[0:WP], low_b[0:WP], thr[:, 1, g:g + 1], up[0:WP],
                                                      ALU.is_lt, ALU.mult))
                        done(dve.tensor_reduce(found[:, 1, g:g + 1], scratch[0:WP], AX.X, ALU.max))
                    done(dve.tensor_scalar(found[:, 0, :], found[:, 0, :], -1.0, float(ET), ALU.mult, ALU.add))
                    done(dve.scalar_tensor_tensor(found[:, 1, :], found[:, 0, :], 1.0, found[:, 1, :], ALU.add, ALU.max))
                    done(dve.tensor_copy(table[:, :, 0], found[:, 0, :]))
                    dve.tensor_copy(table[:, :, 1], found[:, 1, :]).then_inc(e_table, 1)

                @block.tensor
                def _(pe):
                    for g in range(8):
                        r, j0, k = g // 4, 4 * (g % 4), min(4, EJ - 4 * (g % 4))
                        rows = (key_r, slo_r)[r]
                        if g == 0:
                            pe.wait_ge(e_dve, 8)
                        if g == 4:
                            pe.wait_ge(e_dve, 10)
                        for j in range(k):
                            mm = pe.transpose(tp[g][:, j, :], rows[:, (j0 + j) * P:(j0 + j + 1) * P], ident[:])
                        mm.then_inc(e_tr, 1)

        pw = [ps(f"pw{i}", [P, 2, 512], F32) for i in range(2)]
        pd = ps("pd", [P, 512], F32)
        hot, used, win, evac, passed, deg, degout = (sem(n) for n in (
            "hot", "used", "win", "evac", "passed", "deg", "degout"))
        stored = [sem(f"stored{i}") for i in range(2)]

        def load_ranges(e, w4):
            regs = [e.alloc_register(f"range{i}_{nc.next_id()}") for i in range(2 * LW)]
            e.reg_load(regs, ranges[0:1, bass.ds(w4 * 2 * LW, 2 * LW)])
            return regs

        with nc.Block() as block:
            @block.vector
            def _(dve):
                item = dve.alloc_register("item")
                slot_h = dve.alloc_register("slot_h")
                dve.reg_mov(item, 1)
                with dve.Fori(0, WINDOWS // LW) as w4:
                    regs = load_ranges(dve, w4)
                    for u in range(LW):
                        with dve.Fori(regs[2 * u], regs[2 * u + 1]) as t:
                            now = dve.snap(item)
                            slot = dve.snap(now & (RING - 1), min_val=0, max_val=RING - 1)
                            tt = dve.snap(t, min_val=0, max_val=ET - 1)
                            dve.wait_ge(used, now)
                            dve.tensor_scalar(olo[:, bass.ds(slot * P, P)], iota16[:, 0:P], slo_t[:, bass.ds(tt, 1)],
                                              None, ALU.is_equal).then_inc(hot, 1)
                            dve.tensor_scalar(ohi[:, bass.ds(slot * WC, WC)], iota16[:], key_t[:, bass.ds(tt, 1)],
                                              base[:, bass.ds(w4 * LW + u, 1)], ALU.subtract, ALU.is_equal).then_inc(hot, 1)
                            dve.reg_add(item, item, 1)

            @block.tensor
            def _(pe):
                pe.sem_inc(used, RING)
                item = pe.alloc_register("pitem")
                pe.reg_mov(item, 1)

                def windows(first, q, degree):
                    w4 = first + q
                    regs = load_ranges(pe, w4)
                    for u in range(LW):
                        b = u % 2
                        v = pe.snap(w4 * LW + u)
                        pe.wait_ge(evac, v + 1)
                        lhs = place[:, bass.ds(P - W - (v & (P // W - 1)) * W, P)]
                        hi = pe.snap(TILES - (v >> 3))
                        for h in range(2):
                            pe.matmul(pw[b][:, h, 0:WB], lhs, spread[:, h, bass.ds(hi, WB)],
                                      start=True, stop=False, skip_group_check=True)
                        with pe.Fori(regs[2 * u], regs[2 * u + 1]) as t:
                            now = pe.snap(item)
                            slot = pe.snap(now & (RING - 1), min_val=0, max_val=RING - 1)
                            pe.wait_ge(hot, now * 2)
                            for h in range(2):
                                mm = pe.matmul(pw[b][:, h, 0:WB], olo[:, bass.ds(slot * P, P)],
                                               ohi[:, bass.ds(slot * WC + h * WB, WB)], start=False, stop=False,
                                               skip_group_check=True)
                            mm.then_inc(used, 1)
                            pe.reg_add(item, item, 1)
                        pe.matmul(pw[b][:, 1, 0:1], zeros16[:, 0:P], zeros16[:, 0:1], start=False, stop=True,
                                  skip_group_check=True).then_inc(win, 1)
                    if degree is not None:
                        for k in range(KC):
                            mm = pe.matmul(pd[:, 0:BLK], ones16[:], blocks16[degree][:, bass.ds(q * KC + k, 1), :]
                                           .rearrange("p o d -> p (o d)"), start=False, stop=False, skip_group_check=True)
                        mm.then_inc(deg, 1)

                def start_degree(b):
                    pe.wait_ge(evac, pe.snap(b * BW + BW + 2))
                    pe.wait_ge(degout, pe.snap(b + 1))
                    pe.matmul(pd[:, 0:BLK], zeros16[:, 0:P], zeros16[:], start=True, stop=False,
                              skip_group_check=True)

                with pe.Fori(0, CHUNKS) as q:
                    windows(0, q, None)
                with pe.Fori(0, PAIRS - 1) as pair:
                    for par in range(2):
                        b = pe.snap(pair * 2 + par)
                        start_degree(b)
                        with pe.Fori(0, CHUNKS) as q:
                            windows(pe.snap((b + 1) * CHUNKS), q, par)
                start_degree(BLOCKS - 2)
                with pe.Fori(0, CHUNKS) as q:
                    windows((BLOCKS - 1) * CHUNKS, q, 0)
                start_degree(BLOCKS - 1)
                for k in range(TILES):
                    mm = pe.matmul(pd[:, 0:BLK], ones16[:], blocks16[1][:, k, :], start=False, stop=False,
                                   skip_group_check=True)
                mm.then_inc(deg, CHUNKS)

            @block.scalar
            def _(act):
                act.sem_inc(evac, 2)
                act.sem_inc(degout, 1)
                act.preload_act_table(ACT.Identity)

                def window(b, par, q, u):
                    v = act.snap(b * BW + q * 2 + u)
                    act.wait_ge(win, v + 1)
                    act.activation(
                        blocks16[par][:, :, bass.ds(q * 2 * W + u * W, W)].rearrange("p s (h d) -> p s h d", h=2),
                        pw[u][:, :, 0:WB].rearrange("p h (d s) -> p s h d", s=TILES), ACT.Copy,
                        scale=ASCALE).then_inc(evac, 1)

                def degrees(b):
                    act.wait_ge(deg, act.snap(b * CHUNKS + CHUNKS))
                    act.activation(dinv_row[:, bass.ds(b * BLK, BLK)], pd[:, 0:BLK], ACT.Copy,
                                   scale=1.0 / ASCALE).then_inc(degout, 1)

                for par in range(2):
                    with act.Fori(0, BW // 2) as q:
                        for u in range(2):
                            window(par, par, q, u)
                    if par == 1:
                        degrees(0)
                with act.Fori(1, PAIRS) as pair:
                    for par in range(2):
                        act.wait_ge(stored[par], act.snap(pair * 16))
                        with act.Fori(0, BW // 2) as q:
                            for u in range(2):
                                window(act.snap(pair * 2 + par), par, q, u)
                        degrees(act.snap(pair * 2 + par - 1))
                degrees(BLOCKS - 1)

            @block.sync
            def _(sp):
                with sp.Fori(0, PAIRS) as pair:
                    for par in range(2):
                        b = sp.snap(pair * 2 + par)
                        sp.wait_ge(evac, sp.snap(b * BW + BW + 2))
                        sp.sem_inc(passed, 1)
                        sp.dma_start(adj[bass.ds(b, 1)].rearrange("o p n -> (o p) n"),
                                     blocks16[par].rearrange("p s d -> p (s d)")).then_inc(stored[par], 16)
                for par in range(2):
                    sp.wait_ge(stored[par], PAIRS * 16)

        r_step, r_root = sem("r_step"), sem("r_root")
        with nc.Block() as block:
            @block.scalar
            def _(act):
                act.activation(dinv_row[:], dinv_row[:], ACT.Sqrt).then_inc(r_root, 1)

            @block.vector
            def _(dve):
                dve.wait_ge(r_root, 1)
                prod = feat[:].rearrange("p f n -> p (f n)")[:, 0:NP].rearrange("p (t c) -> p t c", t=TILES)
                dve.reciprocal(dinv_row[:], dinv_row[:]).then_inc(r_step, 1)
                dve.wait_ge(r_step, 1)
                dve.tensor_tensor(prod, dinv_row[:].rearrange("p (t c) -> p t c", t=TILES),
                                  ident[:].unsqueeze(1).broadcast_to([P, TILES, P]), ALU.mult).then_inc(r_step, 1)
                dve.wait_ge(r_step, 2)
                dve.tensor_reduce(dinv_col[:], prod, AX.X, ALU.add)


def load_and_norm(nc, sem, x, nodes, feat, ident, mean, rstd, stage):
    with ExitStack() as ctx:
        stats = ctx.enter_context(nc.sbuf_tensor("stats", [P, TILES, BN], F32))
        aggr = ctx.enter_context(nc.sbuf_tensor("aggr", [P, TILES, 2], F32))
        tp = [ctx.enter_context(nc.psum_tensor(f"xt{i}", [P, D], F32)) for i in range(2)]
        l_pad, l_x, l_st, l_root, l_dve, l_n, l_t, l_o = (sem(n) for n in ("l_pad", "l_x", "l_st", "l_root", "l_dve", "l_n", "l_t", "l_o"))
        full = (TILES - 1) * P
        with nc.Block() as block:
            @block.sync
            def _(sp):
                sp.dma_start(nodes[:, 0:TILES - 1, :], x[0:full, :].rearrange("(t p) d -> p t d", p=P)).then_inc(l_x, 16)
                sp.wait_ge(l_pad, 1)
                sp.dma_start(nodes[0:LAST, TILES - 1, :], x[full:N, :]).then_inc(l_x, 16)

            @block.vector
            def _(dve):
                dve.memset(nodes[:, TILES - 1, :], 0.0).then_inc(l_pad, 1)
                dve.wait_ge(l_x, 32)
                with dve.Fori(0, TILES) as t:
                    dve.bn_stats(stats[:, bass.ds(t, 1), :].rearrange("p o s -> p (o s)"),
                                 nodes[:, bass.ds(t, 1), :].rearrange("p o d -> p (o d)")).then_inc(l_st, 1)
                dve.wait_ge(l_st, TILES)
                for t in range(TILES):
                    dve.bn_aggr(aggr[:, t, :], stats[:, t, :]).then_inc(l_st, 1)
                dve.wait_ge(l_st, 2 * TILES)
                dve.tensor_copy(mean[:], aggr[:, :, 0]).then_inc(l_dve, 1)
                dve.tensor_scalar(rstd[:], aggr[:, :, 1], EPS, None, ALU.add).then_inc(l_dve, 1)
                dve.wait_ge(l_root, 1)
                dve.reciprocal(rstd[:], rstd[:]).then_inc(l_dve, 1)
                dve.wait_ge(l_dve, 3)

                def norm(t, u):
                    dve.wait_ge(l_t, t + 1)
                    dve.tensor_scalar(stage[:, u], nodes[:, bass.ds(t, 1), :].rearrange("p o d -> p (o d)"),
                                      mean[:, bass.ds(t, 1)], rstd[:, bass.ds(t, 1)], ALU.subtract,
                                      ALU.mult).then_inc(l_n, 1)

                with dve.Fori(0, TILES // 2) as q:
                    for u in range(2):
                        norm(dve.snap(q * 2 + u), u)
                norm(TILES - 1, 0)

            @block.tensor
            def _(pe):
                pe.sem_inc(l_t, 2)

                def turn(t, u):
                    pe.wait_ge(l_n, t + 1)
                    pe.wait_ge(l_o, t + 1)
                    for f in range(HALVES):
                        mm = pe.transpose(tp[u][:, f * P:(f + 1) * P], stage[:, u, f * P:(f + 1) * P], ident[:])
                    mm.then_inc(l_t, 1)

                with pe.Fori(0, TILES // 2) as q:
                    for u in range(2):
                        turn(pe.snap(q * 2 + u), u)
                turn(TILES - 1, 0)

            @block.scalar
            def _(act):
                act.sem_inc(l_o, 2)
                act.wait_ge(l_dve, 2)
                act.activation(rstd[:], rstd[:], ACT.Sqrt).then_inc(l_root, 1)
                act.preload_act_table(ACT.Identity)

                def put(t, u):
                    act.wait_ge(l_t, t + 3)
                    act.activation(feat[:, :, bass.ds(t * P, P)], tp[u][:].rearrange("p (f n) -> p f n", f=HALVES),
                                   ACT.Copy).then_inc(l_o, 1)

                with act.Fori(0, TILES // 2) as q:
                    for u in range(2):
                        put(act.snap(q * 2 + u), u)
                put(TILES - 1, 0)


def layer(nc, sem, l, adj, feat, hh, chunk, dinv_row, dinv_col, gw_sb, gb_sb, small, smalli, stage):
    relu = l < 2
    with ExitStack() as ctx:
        hp = [ctx.enter_context(nc.psum_tensor(f"hp{l}_{i}", [P, D], F32)) for i in range(2)]
        g_st, g_mm, g_h = (sem(f"{n}{l}") for n in ("g_staged", "g_product", "g_h"))
        m_v, m_p, m_s, m_hi, m_lo = (sem(f"{n}{l}") for n in ("m_max", "m_all", "m_scale", "m_hi", "m_lo"))
        pmax, amax, scale, unscale = (small[:, i:i + 1] for i in range(4))
        expo = smalli[:, 0:1]
        with nc.Block() as block:
            @block.scalar
            def _(act):
                act.preload_act_table(ACT.Identity)

                def put(t, u):
                    act.wait_ge(g_mm, t + 1)
                    act.activation(stage[:, u].rearrange("p (f n) -> p f n", f=HALVES), feat[:, :, bass.ds(t * P, P)],
                                   ACT.Copy).then_inc(g_st, 1)

                with act.Fori(0, TILES // 2) as q:
                    for u in range(2):
                        put(act.snap(q * 2 + u), u)
                put(TILES - 1, 0)
                act.wait_ge(m_v, 5)
                for q in range(CHUNKS):
                    s = slice(q * NP // CHUNKS, (q + 1) * NP // CHUNKS)
                    act.activation(hh[:, 0, :, s], feat[:, :, s], ACT.Copy, scale=scale).then_inc(m_hi, 1)

            @block.tensor
            def _(pe):
                pe.sem_inc(g_mm, 2)

                def product(t, u):
                    pe.wait_ge(g_st, t + 1)
                    pe.wait_ge(g_h, t + 1)
                    for f in range(HALVES):
                        mm = pe.matmul(hp[u][:], stage[:, u, f * P:(f + 1) * P], gw_sb[:, l, f, :],
                                       start=f == 0, stop=f == HALVES - 1)
                    mm.then_inc(g_mm, 1)

                with pe.Fori(0, TILES // 2) as q:
                    for u in range(2):
                        product(pe.snap(q * 2 + u), u)
                product(TILES - 1, 0)

            @block.vector
            def _(dve):
                dve.sem_inc(g_h, 2)

                def put(t, u):
                    dve.wait_ge(g_mm, t + 3)
                    dve.tensor_scalar(feat[:, :, bass.ds(t * P, P)], hp[u][:].rearrange("p (f n) -> p f n", f=HALVES),
                                      dinv_col[:, bass.ds(t, 1)], None, ALU.mult).then_inc(g_h, 1)

                with dve.Fori(0, TILES // 2) as q:
                    for u in range(2):
                        put(dve.snap(q * 2 + u), u)
                put(TILES - 1, 0)
                dve.wait_ge(g_h, TILES + 2)
                dve.tensor_reduce(pmax, feat[:].rearrange("p f n -> p (f n)"), AX.X, ALU.max,
                                  apply_absolute_value=True).then_inc(m_v, 1)
                dve.wait_ge(m_p, 1)
                dve.tensor_scalar(amax, amax, 2.0 ** -90, None, ALU.max).then_inc(m_v, 1)
                dve.wait_ge(m_v, 2)
                dve.tensor_scalar(expo, amax.bitcast(I32), 0x7F800000, None, ALU.bitwise_and).then_inc(m_v, 1)
                dve.wait_ge(m_v, 3)
                dve.tensor_scalar(scale.bitcast(I32), expo, -1.0, float((127 + 127 + 13) << 23), ALU.mult,
                                  ALU.add).then_inc(m_v, 1)
                dve.tensor_scalar(unscale, expo.bitcast(F32), 2.0 ** -13 / ASCALE, None, ALU.mult).then_inc(m_v, 1)
                dve.wait_ge(m_v, 5)
                for q in range(CHUNKS):
                    dve.wait_ge(m_hi, q + 1)
                    s = slice(q * NP // CHUNKS, (q + 1) * NP // CHUNKS)
                    dve.scalar_tensor_tensor(hh[:, 1, :, s], feat[:, :, s], scale, hh[:, 0, :, s], ALU.mult,
                                             ALU.subtract).then_inc(m_lo, 1)

            @block.gpsimd
            def _(pool):
                pool.wait_ge(m_v, 1)
                pool.partition_all_reduce(amax, pmax, P, RED.max).then_inc(m_p, 1)

    with ExitStack() as ctx:
        ap = [[ctx.enter_context(nc.psum_tensor(f"ap{l}_{i}{f}", [P, 512], F32)) for f in range(HALVES)] for i in range(2)]
        tmp = ctx.enter_context(nc.sbuf_tensor(f"tmp{l}", [P, 2, HALVES, BLK], F32))
        a_in = [sem(f"a_in{l}_{k}") for k in range(CHUNKS)]
        a_used, a_passed, a_scaled, a_out = (sem(f"{n}{l}") for n in ("a_used", "a_passed", "a_scaled", "a_out"))
        unscale = small[:, 3:4]
        with nc.Block() as block:
            @block.sync
            def _(sp):
                def fetch(b):
                    for k in range(CHUNKS):
                        if not isinstance(b, int):
                            sp.wait_ge(a_used, sp.snap(b * CHUNKS - CHUNKS + k + 1, min_val=1))
                            sp.sem_inc(a_passed, 1)
                        sp.dma_start(chunk[:, k].rearrange("p k d -> p (k d)"),
                                     adj[bass.ds(b, 1), :, k * KC * BLK:(k + 1) * KC * BLK]
                                     .rearrange("o p n -> (o p) n")).then_inc(a_in[k], 16)

                fetch(0)
                with sp.Fori(1, BLOCKS) as b:
                    fetch(b)

            @block.tensor
            def _(pe):
                with pe.Fori(0, PAIRS) as pair:
                    for par in range(2):
                        b = pe.snap(pair * 2 + par)
                        pe.wait_ge(a_scaled, b * HALVES + 1)
                        pe.wait_ge(a_scaled, b * HALVES + 2)
                        for k in range(TILES):
                            if k % KC == 0:
                                pe.wait_ge(a_in[k // KC], b * 16 + 16)
                            for f in range(HALVES):
                                for q in range(2):
                                    mm = pe.matmul(ap[par][f][:, 0:BLK], hh[:, q, f, k * P:(k + 1) * P],
                                                   chunk[:, k // KC, k % KC, :], start=(k == 0 and q == 0),
                                                   stop=(k == TILES - 1 and q == 1))
                            if k % KC == KC - 1:
                                mm.then_inc(a_used, 1)

            @block.vector
            def _(dve):
                dve.sem_inc(a_scaled, 2 * HALVES)

                with dve.Fori(0, PAIRS) as pair:
                    for par in range(2):
                        b = dve.snap(pair * 2 + par)
                        dve.wait_ge(a_used, b * CHUNKS + CHUNKS)
                        for f in range(HALVES):
                            dve.wait_ge(a_out, b * HALVES + f + 1)
                            dve.tensor_tensor(tmp[:, par, f], ap[par][f][:, 0:BLK], dinv_row[:, bass.ds(b * BLK, BLK)],
                                              ALU.mult).then_inc(a_scaled, 1)

            @block.scalar
            def _(act):
                act.sem_inc(a_out, 2 * HALVES)
                act.preload_act_table(ACT.Identity)
                with act.Fori(0, PAIRS) as pair:
                    for par in range(2):
                        b = act.snap(pair * 2 + par)
                        for f in range(HALVES):
                            act.wait_ge(a_scaled, b * HALVES + f + 1 + 2 * HALVES)
                            act.activation(feat[:, f, bass.ds(b * BLK, BLK)], tmp[:, par, f],
                                           ACT.Relu if relu else ACT.Identity, bias=gb_sb[:, l, f:f + 1],
                                           scale=unscale).then_inc(a_out, 1)


def finish(nc, sem, x, nodes, feat, big_b, dinv_row, ident, ones, mean, rstd, stage, small, route_row,
           wr, br, w1, b1, w2, b2, out):
    full = (TILES - 1) * P
    with ExitStack() as ctx:
        def sb(name, shape, dt):
            return ctx.enter_context(nc.sbuf_tensor(name, shape, dt))

        free = big_b[:].bitcast(F32)
        w1_sb = sb("w1_sb", [P, HALVES, HID], F32)
        w2_sb = free[:, 0:HM * D].rearrange("p (m n) -> p m n", m=HM)
        hid_flat = free[:, HM * D:HM * D + HM * 7 * P]
        hid = hid_flat.rearrange("p (m n) -> p m n", m=HM)
        stats = sb("fstats", [P, TILES, BN], F32)
        aggr = sb("faggr", [P, TILES, 2], F32)
        wr_b = sb("wr_b", [P, D], F32)
        b2_b = sb("b2_b", [P, D], F32)
        b1_sb = sb("b1_sb", [P, HM], F32)
        br_b = sb("br_b", [P, 1], F32)
        route = sb("route", [P, TILES], F32)
        turned = sb("turned", [TILES, P], F32)
        xn = sb("xn", [P, 2, D], F32)
        junk = sb("junk", [P, D], F32)
        psz = [ctx.enter_context(nc.psum_tensor(f"fp{i}", [P, 512], F32)) for i in range(8)]
        f_w, f_pad, f_x, f_g, f_t, f_x1, f_st, f_v, f_root = (sem(n) for n in ("f_w", "f_pad", "f_x", "f_g", "f_t", "f_x1", "f_st", "f_v", "f_root"))
        with nc.Block() as block:
            @block.sync
            def _(sp):
                sp.dma_start(nodes[:, 0:TILES - 1, :], x[0:full, :].rearrange("(t p) d -> p t d", p=P)).then_inc(f_x, 16)
                sp.dma_start(w1_sb[:], w1.rearrange("(k p) n -> p k n", p=P)).then_inc(f_w, 16)
                sp.dma_start(w2_sb, w2.rearrange("(m p) n -> p m n", p=P)).then_inc(f_w, 16)
                with nc.allow_non_contiguous_dma(reason="small vectors"):
                    sp.dma_start(b1_sb[:], b1.rearrange("(m p) -> p m", p=P)).then_inc(f_w, 16)
                    sp.dma_start(wr_b[:], wr.rearrange("d o -> o d").broadcast_to([P, D])).then_inc(f_w, 16)
                sp.dma_start(b2_b[:], b2.rearrange("(o d) -> o d", o=1).broadcast_to([P, D])).then_inc(f_w, 16)
                sp.dma_start(br_b[:], br.rearrange("(o d) -> o d", o=1).broadcast_to([P, 1])).then_inc(f_w, 16)
                sp.wait_ge(f_pad, 1)
                sp.dma_start(nodes[0:LAST, TILES - 1, :], x[full:N, :]).then_inc(f_x, 16)
                sp.wait_ge(f_w, 96)

            @block.scalar
            def _(act):
                act.preload_act_table(ACT.Identity)
                act.sem_inc(f_t, 2)

                def put(t, u):
                    act.wait_ge(f_t, t + 1)
                    act.activation(stage[:, u].rearrange("p (f n) -> p f n", f=HALVES), feat[:, :, bass.ds(t * P, P)],
                                   ACT.Copy).then_inc(f_g, 1)

                with act.Fori(0, TILES // 2) as q:
                    for u in range(2):
                        put(act.snap(q * 2 + u), u)
                put(TILES - 1, 0)
                act.wait_ge(f_v, 1)
                act.activation(rstd[:], rstd[:], ACT.Sqrt).then_inc(f_root, 1)

            @block.tensor
            def _(pe):
                pe.sem_inc(f_x1, 2)

                def turn(t, u):
                    pe.wait_ge(f_g, t + 1)
                    pe.wait_ge(f_x1, t + 1)
                    for f in range(HALVES):
                        mm = pe.transpose(psz[u][:, f * P:(f + 1) * P], stage[:, u, f * P:(f + 1) * P], ident[:])
                    mm.then_inc(f_t, 1)

                with pe.Fori(0, TILES // 2) as q:
                    for u in range(2):
                        turn(pe.snap(q * 2 + u), u)
                turn(TILES - 1, 0)

            @block.vector
            def _(dve):
                dve.memset(nodes[:, TILES - 1, :], 0.0).then_inc(f_pad, 1)
                dve.wait_ge(f_x, 32)

                def put(t, u):
                    tile = nodes[:, bass.ds(t, 1), :].rearrange("p o d -> p (o d)")
                    dve.wait_ge(f_t, t + 3)
                    dve.tensor_tensor(tile, tile, psz[u][:, 0:D], ALU.add).then_inc(f_x1, 1)

                with dve.Fori(0, TILES // 2) as q:
                    for u in range(2):
                        put(dve.snap(q * 2 + u), u)
                put(TILES - 1, 0)
                dve.wait_ge(f_x1, TILES + 2)
                with dve.Fori(0, TILES) as t:
                    dve.bn_stats(stats[:, bass.ds(t, 1), :].rearrange("p o s -> p (o s)"),
                                 nodes[:, bass.ds(t, 1), :].rearrange("p o d -> p (o d)")).then_inc(f_st, 1)
                dve.wait_ge(f_st, TILES)
                for t in range(TILES):
                    dve.bn_aggr(aggr[:, t, :], stats[:, t, :]).then_inc(f_st, 1)
                dve.wait_ge(f_st, 2 * TILES)
                dve.tensor_copy(mean[:], aggr[:, :, 0])
                dve.tensor_scalar(rstd[:], aggr[:, :, 1], EPS, None, ALU.add).then_inc(f_v, 1)
                dve.wait_ge(f_root, 1)
                dve.reciprocal(rstd[:], rstd[:])

        n_x, n_t, n_o, n_r, n_b = (sem(n) for n in ("n_x", "n_t", "n_o", "n_r", "n_b"))
        with nc.Block() as block:
            @block.vector
            def _(dve):
                def one(t, u):
                    tile = nodes[:, bass.ds(t, 1), :].rearrange("p o d -> p (o d)")
                    dve.wait_ge(n_t, t + 1)
                    dve.tensor_scalar(xn[:, u], tile, mean[:, bass.ds(t, 1)], rstd[:, bass.ds(t, 1)], ALU.subtract,
                                      ALU.mult).then_inc(n_x, 1)
                    dve.wait_ge(n_x, t + 1)
                    dve.scalar_tensor_tensor(junk[:], xn[:, u], 1.0, wr_b[:], ALU.mult, ALU.mult,
                                             accum_out=route[:, bass.ds(t, 1)]).then_inc(n_r, 1)
                    dve.tensor_tensor(tile, tile, xn[:, u], ALU.add).then_inc(n_b, 1)
                    dve.wait_ge(n_r, t + 1)

                with dve.Fori(0, TILES // 2) as q:
                    for u in range(2):
                        one(dve.snap(q * 2 + u), u)
                one(TILES - 1, 0)
                dve.tensor_scalar(route[:], route[:], br_b[:], None, ALU.add).then_inc(n_r, 1)

            @block.tensor
            def _(pe):
                pe.sem_inc(n_t, 2)

                def turn(t, u):
                    pe.wait_ge(n_x, t + 1)
                    pe.wait_ge(n_o, t + 1)
                    pe.wait_ge(n_b, t + 1)
                    pe.wait_ge(n_r, t + 1)
                    for f in range(HALVES):
                        mm = pe.transpose(psz[u][:, f * P:(f + 1) * P], xn[:, u, f * P:(f + 1) * P], ident[:])
                    mm.then_inc(n_t, 1)

                with pe.Fori(0, TILES // 2) as q:
                    for u in range(2):
                        turn(pe.snap(q * 2 + u), u)
                turn(TILES - 1, 0)
                pe.wait_ge(n_r, TILES + 1)
                pe.transpose(psz[2][0:TILES, 0:P], route[:], ident[:]).then_inc(n_t, 1)

            n_w, n_d = sem("n_w"), sem("n_d")

            @block.scalar
            def _(act):
                act.sem_inc(n_o, 2)
                act.preload_act_table(ACT.Identity)

                def put(t, u):
                    act.wait_ge(n_t, t + 3)
                    act.activation(feat[:, :, bass.ds(t * P, P)], psz[u][:, 0:D].rearrange("p (f n) -> p f n", f=HALVES),
                                   ACT.Copy).then_inc(n_o, 1)

                with act.Fori(0, TILES // 2) as q:
                    for u in range(2):
                        put(act.snap(q * 2 + u), u)
                put(TILES - 1, 0)
                act.wait_ge(n_t, TILES + 3)
                act.activation(turned[:], psz[2][0:TILES, 0:P], ACT.Copy).then_inc(n_w, 1)

            @block.sync
            def _(sp):
                sp.wait_ge(n_w, 1)
                sp.dma_start(route_row, turned[:]).then_inc(n_d, 16)
                sp.wait_ge(n_d, 16)
                sp.dma_start(dinv_row[:], route_row.rearrange("(o t) p -> o (t p)", o=1).broadcast_to([P, NP])).then_inc(n_d, 16)
                sp.wait_ge(n_d, 32)

        more = sb("more", [P, TILES], F32)
        cand = sb("cand", [P, TILES], F32)
        tie = sb("tie", [P, TILES], F32)
        tri = sb("tri", [P, P], F32)
        before = sb("before", [P, TILES], F32)
        col = sb("col", [P, TILES], F32)
        ahead = sb("ahead", [P, TILES], F32)
        gate = sb("gate", [P, TILES], F32)
        idx_i = sb("idx_i", [P, TILES], I32)
        real = sb("real", [P, TILES], F32)
        zero49 = sb("zero49", [P, TILES], F32)
        best, allbest, room = (small[:, i:i + 1] for i in (8, 9, 10))
        s_c, s_v, s_p, s_m, s_g = (sem(n) for n in ("s_c", "s_v", "s_p", "s_m", "s_g"))
        h_mm, h_act, y_mm, y_out, o_dma = (sem(n) for n in ("h_mm", "h_act", "y_mm", "y_out", "o_dma"))
        y_t = sem("y_t")
        o_passed = sem("o_passed")
        rows = feat[:].rearrange("p f n -> p (f n)")
        work = hid_flat[:, 0:N // 2]
        with nc.Block() as block:
            @block.gpsimd
            def _(pool):
                pool.iota(idx_i[:], pattern=[[P, TILES]], base=0, channel_multiplier=1).then_inc(s_c, 1)
                pool.memset(tri[:], 1.0).then_inc(s_c, 1)
                pool.wait_ge(s_c, 2)
                pool.affine_select(out=tri[:], in_=tri[:], compare_op=ALU.is_gt, fill=0.0, base=0,
                                   pattern=[[1, P]], channel_multiplier=-1).then_inc(s_c, 1)
                pool.wait_ge(s_p, 1)
                pool.partition_all_reduce(allbest, best, P, RED.max).then_inc(s_p, 1)

            @block.vector
            def _(dve):
                n = [0]

                def done(ins):
                    n[0] += 1
                    ins.then_inc(s_v, 1)
                    dve.wait_ge(s_v, n[0])

                dve.wait_ge(s_c, 3)
                done(dve.tensor_scalar(real[:], idx_i[:], float(N), None, ALU.is_lt))
                done(dve.memset(zero49[:], 0.0))
                half = N // 2
                for t in range(TILES):
                    for h in range(2):
                        done(dve.tensor_scalar(work, dinv_row[:, h * half:(h + 1) * half], route[:, t:t + 1],
                                               0.0, ALU.is_gt, ALU.add, accum_out=(more, col)[h][:, t:t + 1]))
                done(dve.tensor_tensor(more[:], more[:], col[:], ALU.add))
                done(dve.scalar_tensor_tensor(cand[:], more[:], float(KEEP), real[:], ALU.is_lt, ALU.mult))
                done(dve.scalar_tensor_tensor(before[:], more[:], 1.0, cand[:], ALU.add, ALU.mult))
                dve.tensor_reduce(best, before[:], AX.X, ALU.max).then_inc(s_p, 1)
                dve.wait_ge(s_p, 2)
                done(dve.tensor_scalar(tie[:], before[:], allbest, None, ALU.is_equal))
                done(dve.tensor_scalar(room, allbest, -1.0, float(KEEP + 1), ALU.mult, ALU.add))
                dve.wait_ge(s_m, 1)
                done(dve.tensor_copy(col[:], psz[7][:, 64:64 + TILES]))
                done(dve.tensor_tensor_scan(ahead[:], col[:], zero49[:], 0.0, ALU.add, ALU.add))
                done(dve.tensor_tensor(ahead[:], ahead[:], col[:], ALU.subtract))
                done(dve.tensor_tensor(ahead[:], ahead[:], psz[7][:, 0:TILES], ALU.add))
                done(dve.scalar_tensor_tensor(ahead[:], ahead[:], room, tie[:], ALU.is_ge, ALU.mult))
                done(dve.tensor_tensor(cand[:], cand[:], ahead[:], ALU.subtract))
                done(dve.tensor_tensor(gate[:], cand[:], route[:], ALU.mult))

                with dve.Fori(0, 7) as c:
                    for i in range(7):
                        t = dve.snap(c * 7 + i)
                        tile = nodes[:, bass.ds(t, 1), :].rearrange("p o d -> p (o d)")
                        dve.wait_ge(y_mm, t + 2)
                        dve.tensor_tensor(xn[:, i % 2], psz[4 + i % 2][:, 0:D], b2_b[:], ALU.add).then_inc(y_t, 1)
                        dve.wait_ge(y_t, t + 2)
                        dve.scalar_tensor_tensor(tile, xn[:, i % 2], gate[:, bass.ds(t, 1)], tile, ALU.mult,
                                                 ALU.add).then_inc(y_out, 1)
                        dve.wait_ge(y_out, t + 1)

            @block.tensor
            def _(pe):
                pe.sem_inc(h_act, 4)
                pe.sem_inc(y_mm, 1)
                pe.sem_inc(y_t, 1)

                def ranks():
                    pe.wait_ge(s_v, 2 + 2 * TILES + 4)
                    pe.matmul(psz[7][:, 0:TILES], tri[:], tie[:], start=True, stop=True)
                    pe.matmul(psz[7][:, 64:64 + TILES], ones[:], tie[:], start=True, stop=True,
                              skip_group_check=True).then_inc(s_m, 1)

                def hidden(c, m):
                    for g in range(2):
                        r = (2 * m + g) % 4
                        pe.wait_ge(h_act, c * 2 * HM + 2 * m + g + 1)
                        for k in range(HALVES):
                            mm = pe.matmul(psz[r][:, 0:BLK], w1_sb[:, k, m * P:(m + 1) * P],
                                           feat[:, k, bass.ds(c * 2 * BLK + g * BLK, BLK)], start=k == 0,
                                           stop=k == HALVES - 1)
                        mm.then_inc(h_mm, 1)

                ranks()
                with pe.Fori(0, 7) as c:
                    for m in range(HM):
                        hidden(c, m)
                    pe.wait_ge(h_act, c * 2 * HM + 2 * HM + 4)
                    for i in range(7):
                        t = pe.snap(c * 7 + i)
                        pe.wait_ge(y_t, t + 1 if i == 0 else t)
                        for m in range(HM):
                            mm = pe.matmul(psz[4 + i % 2][:, 0:D], hid[:, m, i * P:(i + 1) * P], w2_sb[:, m, :],
                                           start=m == 0, stop=m == HM - 1)
                        mm.then_inc(y_mm, 1)

            @block.scalar
            def _(act):
                act.preload_act_table(ACT.Gelu_apprx_tanh)
                with act.Fori(0, 7) as c:
                    for m in range(HM):
                        for g in range(2):
                            r = (2 * m + g) % 4
                            act.wait_ge(h_mm, c * 2 * HM + 2 * m + g + 1)
                            if m == 0 and g == 0:
                                act.wait_ge(y_mm, c * 7 + 1)
                            act.activation(hid[:, m, g * BLK:(g + 1) * BLK], psz[r][:, 0:BLK], ACT.Gelu_apprx_tanh,
                                           bias=b1_sb[:, m:m + 1]).then_inc(h_act, 1)

            @block.sync
            def _(sp):
                with sp.Fori(0, 6) as c:
                    sp.wait_ge(y_out, c * 7 + 7)
                    sp.sem_inc(o_passed, 1)
                    sp.dma_start(out[bass.ds(c * 7 * P, 7 * P), :].rearrange("(t p) d -> p t d", p=P),
                                 nodes[:, bass.ds(c * 7, 7), :]).then_inc(o_dma, 16)
                sp.wait_ge(y_out, TILES)
                sp.dma_start(out[42 * P:48 * P, :].rearrange("(t p) d -> p t d", p=P), nodes[:, 42:48, :]).then_inc(o_dma, 16)
                sp.dma_start(out[48 * P:N, :], nodes[0:LAST, 48, :]).then_inc(o_dma, 16)
                sp.wait_ge(o_dma, 8 * 16)


_INS = ["x", "src", "dst", "L0_gnn_W1", "L0_gnn_b1", "L0_gnn_W2", "L0_gnn_b2", "L0_gnn_W3", "L0_gnn_b3",
        "L0_ffn_wr", "L0_ffn_br", "L0_ffn_w1", "L0_ffn_b1", "L0_ffn_w2", "L0_ffn_b2"]


def kernel(**inputs):
    import concourse.bacc as bacc
    from concourse.bass_utils import run_bass_kernel_spmd

    nc = bacc.Bacc("TRN2", target_bir_lowering=False, num_devices=1)
    arrays, a = {}, {}
    for name in _INS:
        array = np.ascontiguousarray(inputs[name])
        arrays[f"in_{name}"] = array
        a[name] = nc.dram_tensor(f"in_{name}", array.shape, mybir.dt.from_np(array.dtype), kind="ExternalInput").ap()
    out = nc.dram_tensor("out", (N, D), F32, kind="ExternalOutput").ap()
    build(nc, a["x"], a["src"], a["dst"], [a[f"L0_gnn_W{i}"] for i in (1, 2, 3)], [a[f"L0_gnn_b{i}"] for i in (1, 2, 3)],
          a["L0_ffn_wr"], a["L0_ffn_br"], a["L0_ffn_w1"], a["L0_ffn_b1"], a["L0_ffn_w2"], a["L0_ffn_b2"], out)
    r = run_bass_kernel_spmd(nc, [arrays], core_ids=[0])
    return r.results[0]["out"]
```

```python
from contextlib import ExitStack

import numpy as np
import concourse.bass as bass
from concourse import mybir

ALU = mybir.AluOpType
ACT = mybir.ActivationFunctionType
AX = mybir.AxisListType
F32 = mybir.dt.float32
F16 = mybir.dt.float16
I32 = mybir.dt.int32
RED = bass.bass_isa.ReduceOp

P = 128
D = 256
HALVES = D // P
N = 6250
TILES = -(-N // P)
NP = TILES * P
LAST = N - (TILES - 1) * P
E = 200000
EJ = 13
ET = P * EJ
EFULL = E // (EJ * P)
EREST = E - EFULL * EJ * P
W = 16
HW = W // 2
WB = HW * TILES
WC = 2 * WB
WINDOWS = NP // W
WP = 98
WG = WINDOWS // WP
BLK = 448
BLOCKS = NP // BLK
PAIRS = BLOCKS // 2
BW = BLK // W
GW = P // W
HG = GW // 2
PT = 2
KC = 7
CHUNKS = TILES // KC
PAD = 8191
HID = 4 * D
HM = HID // P
KEEP = max(1, int(0.5 * N)) - 1
ASCALE = 0.25
EPS = 1e-5
BN = 6


def build(nc, x, src, dst, gw, gb, wr, br, w1, b1, w2, b2, out):
    ctx = ExitStack()
    with ctx:
        def sb(name, shape, dt):
            return ctx.enter_context(nc.sbuf_tensor(name, shape, dt))

        def sem(name):
            return ctx.enter_context(nc.semaphore(name))

        adj = nc.dram_tensor("adj", (BLOCKS, P, TILES * BLK), F16, kind="Internal").ap()
        tile_ends = nc.dram_tensor("tile_ends", (2, ET), F32, kind="Internal").ap()
        route_row = nc.dram_tensor("route_row", (TILES, P), F32, kind="Internal").ap()

        big_a = sb("big_a", [P, TILES * D], F32)
        big_b = sb("big_b", [P, TILES * BLK], F16)
        feat = sb("feat", [P, HALVES, NP], F32)
        dinv_all = sb("dinv_all", [P, BLK + NP], F32)
        dinv_row = dinv_all[:, BLK:BLK + NP]
        dinv_col = sb("dinv_col", [P, TILES], F32)
        ident = sb("ident", [P, P], F32)
        ones = sb("ones", [P, P], F32)
        ones16 = sb("ones16", [P, P], F16)
        stage = sb("stage", [P, 2, D], F32)
        gw_sb = sb("gw_sb", [P, 3, HALVES, D], F32)
        gb_sb = sb("gb_sb", [P, 3, HALVES], F32)
        small = sb("small", [P, 64], F32)
        smalli = sb("smalli", [P, 8], I32)
        mean = sb("mean", [P, TILES], F32)
        rstd = sb("rstd", [P, TILES], F32)
        hh = big_a[:].bitcast(F16).rearrange("p (q f n) -> p q f n", q=2, f=HALVES)
        blocks16 = [big_a[:].bitcast(F16)[:, 0:TILES * BLK].rearrange("p (s d) -> p s d", s=TILES),
                    big_b[:].rearrange("p (s d) -> p s d", s=TILES)]
        chunk = big_b[:].rearrange("p (c k d) -> p c k d", c=CHUNKS, k=KC)
        nodes = big_a[:].rearrange("p (t d) -> p t d", t=TILES)

        c_init = sem("c_init")

        with nc.Block() as block:
            @block.gpsimd
            def _(pool):
                pool.memset(ident[:], 0.0).then_inc(c_init, 1)
                pool.wait_ge(c_init, 1)
                pool.affine_select(out=ident[:], in_=ident[:], compare_op=ALU.not_equal, fill=1.0, base=0,
                                   pattern=[[-1, P]], channel_multiplier=1).then_inc(c_init, 1)

            @block.vector
            def _(dve):
                dve.memset(ones[:], 1.0)
                dve.memset(ones16[:], 1.0)

            @block.sync
            def _(sp):
                s = sem("s_weights")
                for l in range(3):
                    sp.dma_start(gw_sb[:, l], gw[l].rearrange("(k p) n -> p k n", p=P)).then_inc(s, 16)
                    with nc.allow_non_contiguous_dma(reason="a bias of 256 values"):
                        sp.dma_start(gb_sb[:, l], gb[l].rearrange("(k p) -> p k", p=P)).then_inc(s, 16)
                sp.wait_ge(s, 96)

        build_adjacency(nc, sem, src, dst, adj, tile_ends, big_a, big_b, dinv_all, dinv_col, feat, ident, ones16, blocks16)
        load_and_norm(nc, sem, x, nodes, feat, ident, mean, rstd, stage)
        for l in range(3):
            layer(nc, sem, l, adj, feat, hh, chunk, dinv_row, dinv_col, gw_sb, gb_sb, small, smalli, stage)
        finish(nc, sem, x, nodes, feat, big_b, dinv_row, ident, ones, mean, rstd, stage, small, route_row,
               wr, br, w1, b1, w2, b2, out)


def build_adjacency(nc, sem, src, dst, adj, tile_ends, big_a, big_b, dinv_all, dinv_col, feat, ident, ones16, blocks16):
    with ExitStack() as ctx:
        def sb(name, shape, dt):
            return ctx.enter_context(nc.sbuf_tensor(name, shape, dt))

        def ps(name, shape, dt):
            return ctx.enter_context(nc.psum_tensor(name, shape, dt))

        dinv_row = dinv_all[:, BLK:BLK + NP]
        tmp = feat[:].rearrange("p f n -> p (f n)")
        dst_i = tmp[:, 0:ET].bitcast(I32)
        src_i = tmp[:, ET:2 * ET].bitcast(I32)
        dst_f = tmp[:, 2 * ET:3 * ET]
        key_r = tmp[:, 3 * ET:4 * ET]
        slo_r = tmp[:, 4 * ET:5 * ET]
        low_b = tmp[:, 5 * ET:6 * ET]
        high_b = tmp[:, 6 * ET:7 * ET]
        iota_i = dinv_row[:, 0:ET].bitcast(I32)
        up = dinv_row[:, ET:2 * ET]
        down = dinv_row[:, 2 * ET:3 * ET]
        key_t = tmp[:, 0:ET]
        slo_t = tmp[:, ET:2 * ET]
        slots = PT
        ohi = tmp[:, 2 * ET:2 * ET + slots * WC // 2].bitcast(F16)
        olo = tmp[:, 2 * ET + slots * WC // 2:2 * ET + slots * (WC + P) // 2].bitcast(F16)
        scratch = big_a[:, 0:ET]
        iota16 = sb("iota16", [P, WC], F16)
        base = sb("base", [P, WINDOWS], F32)
        own_base = sb("own_base", [P, 2, GW], F32)
        base_i = sb("base_i", [P, WINDOWS], I32)
        thr = sb("thr", [WP, 2, WG], F32)
        thr_i = sb("thr_i", [WP, 2, WG], I32)
        ends = sb("ends", [P, 2, EJ], F32)
        found = sb("found", [WP, 2, WG], F32)
        table = sb("table", [WP, WG, 2], I32)
        ranges = sb("ranges", [1, 2 * WINDOWS], I32)
        zeros16 = sb("zeros16", [P, BLK], F16)
        place = sb("place", [P, 2 * P - W], F16)
        spread = sb("spread", [P, 2, TILES + WB], F16)
        e_pad, e_rows, e_dve, e_pool, e_ends, e_rt, e_tr = (sem(n) for n in (
            "e_pad", "e_rows", "e_dve", "e_pool", "e_ends", "e_roundtrip", "e_transposed"))
        e_zero = sem("e_zero")
        e_bc, e_table, e_tload = sem("e_bc"), sem("e_table"), sem("e_tload")

        with ExitStack() as c2:
            tp = [c2.enter_context(nc.psum_tensor(f"tp{i}", [P, 4, P], F32)) for i in range(8)]
            with nc.Block() as block:
                @block.gpsimd
                def _(pool):
                    pool.iota(iota_i, pattern=[[1, ET]], base=0, channel_multiplier=0).then_inc(e_pool, 1)
                    pool.iota(base_i[:], pattern=[[1, WINDOWS]], base=0, channel_multiplier=0).then_inc(e_pool, 1)
                    pool.iota(thr_i[:, 0, :], pattern=[[W, WG]], base=0, channel_multiplier=W * WG).then_inc(e_pool, 1)
                    pool.iota(thr_i[:, 1, :], pattern=[[W, WG]], base=W, channel_multiplier=W * WG).then_inc(e_pool, 1)
                    pool.memset(place[:], 0.0).then_inc(e_pool, 1)
                    pool.memset(spread[:], 0.0).then_inc(e_pool, 1)
                    pool.memset(zeros16[:], 0.0).then_inc(e_pool, 1)
                    pool.memset(big_b[:].bitcast(F32), 0.0).then_inc(e_zero, 1)
                    pool.wait_ge(e_pool, 7)
                    pool.affine_select(out=place[0:W], in_=place[0:W], compare_op=ALU.not_equal, fill=1.0,
                                       base=P - W, pattern=[[-1, 2 * P - W]], channel_multiplier=1).then_inc(e_pool, 1)
                    for h in range(2):
                        pool.affine_select(out=spread[0:W, h], in_=spread[0:W, h], compare_op=ALU.not_equal, fill=1.0,
                                           base=TILES - HW * h * TILES, pattern=[[-1, TILES + WB]],
                                           channel_multiplier=TILES).then_inc(e_pool, 1)

                @block.sync
                def _(sp):
                    sp.wait_ge(e_pad, 2)
                    rows = lambda a: a[0:EFULL * EJ * P].rearrange("(p e) -> p e", p=EFULL)
                    rest = lambda a: a[EFULL * EJ * P:E].rearrange("(p e) -> p e", p=1)
                    sp.dma_start(dst_i[0:EFULL, :], rows(dst)).then_inc(e_rows, 16)
                    sp.dma_start(dst_i[EFULL:EFULL + 1, 0:EREST], rest(dst)).then_inc(e_rows, 16)
                    sp.dma_start(src_i[0:EFULL, :], rows(src)).then_inc(e_rows, 16)
                    sp.dma_start(src_i[EFULL:EFULL + 1, 0:EREST], rest(src)).then_inc(e_rows, 16)
                    sp.wait_ge(e_ends, 2)
                    sp.dma_start(tile_ends.rearrange("a (p j) -> p a j", p=P), ends[:]).then_inc(e_rt, 16)
                    sp.wait_ge(e_rt, 16)
                    sp.dma_start(low_b, tile_ends[0:1, :].broadcast_to([P, ET])).then_inc(e_bc, 16)
                    sp.dma_start(high_b, tile_ends[1:2, :].broadcast_to([P, ET])).then_inc(e_bc, 16)
                    sp.wait_ge(e_table, 1)
                    sp.dma_start(ranges[0:1, :], table[:].rearrange("p g c -> p (g c)")).then_inc(e_tload, 16)
                    sp.wait_ge(e_tload, 16)

                @block.vector
                def _(dve):
                    n = [0]

                    def done(ins):
                        n[0] += 1
                        ins.then_inc(e_dve, 1)
                        dve.wait_ge(e_dve, n[0])

                    dve.memset(dst_i, PAD).then_inc(e_pad, 1)
                    dve.memset(src_i, 0).then_inc(e_pad, 1)
                    dve.wait_ge(e_pool, 4)
                    done(dve.tensor_copy(iota16[:], iota_i[:, 0:WC]))
                    done(dve.tensor_scalar(base[:], base_i[:], float(-W * TILES), None, ALU.mult))
                    done(dve.tensor_scalar(up, iota_i, 1.0, None, ALU.add))
                    done(dve.tensor_scalar(down, iota_i, -1.0, float(ET), ALU.mult, ALU.add))
                    done(dve.tensor_copy(thr[:], thr_i[:]))
                    dve.wait_ge(e_rows, 64)
                    done(dve.tensor_copy(dst_f, dst_i))
                    rows3 = dst_f.rearrange("p (j e) -> p j e", j=EJ)
                    dve.tensor_reduce(ends[:, 0, :], rows3, AX.X, ALU.min).then_inc(e_ends, 1)
                    dve.tensor_reduce(ends[:, 1, :], rows3, AX.X, ALU.max).then_inc(e_ends, 1)
                    done(dve.tensor_scalar(slo_r.bitcast(I32), src_i, 7, None, ALU.arith_shift_right))
                    done(dve.scalar_tensor_tensor(key_r, dst_f, float(TILES), slo_r.bitcast(I32), ALU.mult, ALU.add))
                    done(dve.tensor_scalar(dst_i, src_i, P - 1, None, ALU.bitwise_and))
                    done(dve.tensor_copy(slo_r, dst_i))
                    for g in range(8):
                        dve.wait_ge(e_tr, g + 1)
                        r, j0, k = g // 4, 4 * (g % 4), min(4, EJ - 4 * (g % 4))
                        t = (key_t, slo_t)[r].rearrange("p (q j) -> p j q", j=EJ)
                        done(dve.tensor_copy(t[:, j0:j0 + k, :], tp[g][:, 0:k, :]))
                    dve.wait_ge(e_bc, 32)
                    for g in range(WG):
                        done(dve.scalar_tensor_tensor(scratch[0:WP], high_b[0:WP], thr[:, 0, g:g + 1], down[0:WP],
                                                      ALU.is_ge, ALU.mult))
                        done(dve.tensor_reduce(found[:, 0, g:g + 1], scratch[0:WP], AX.X, ALU.max))
                        done(dve.scalar_tensor_tensor(scratch[0:WP], low_b[0:WP], thr[:, 1, g:g + 1], up[0:WP],
                                                      ALU.is_lt, ALU.mult))
                        done(dve.tensor_reduce(found[:, 1, g:g + 1], scratch[0:WP], AX.X, ALU.max))
                    done(dve.tensor_scalar(found[:, 0, :], found[:, 0, :], -1.0, float(ET), ALU.mult, ALU.add))
                    done(dve.scalar_tensor_tensor(found[:, 1, :], found[:, 0, :], 1.0, found[:, 1, :], ALU.add, ALU.max))
                    done(dve.tensor_copy(table[:, :, 0], found[:, 0, :]))
                    dve.tensor_copy(table[:, :, 1], found[:, 1, :]).then_inc(e_table, 1)

                @block.tensor
                def _(pe):
                    for g in range(8):
                        r, j0, k = g // 4, 4 * (g % 4), min(4, EJ - 4 * (g % 4))
                        rows = (key_r, slo_r)[r]
                        if g == 0:
                            pe.wait_ge(e_dve, 8)
                        if g == 4:
                            pe.wait_ge(e_dve, 10)
                        for j in range(k):
                            mm = pe.transpose(tp[g][:, j, :], rows[:, (j0 + j) * P:(j0 + j + 1) * P], ident[:])
                        mm.then_inc(e_tr, 1)

        pw = [ps(f"pw{i}", [P, 2, 512], F32) for i in range(2)]
        pd = ps("pd", [P, 512], F32)
        hot, used, win, evac, passed, deg, degout, free, based = (sem(n) for n in (
            "hot", "used", "win", "evac", "passed", "deg", "degout", "free", "based"))
        stored = sem("stored")

        def in_table(e, t):
            return nc.s_assert_within(t, 0, ET - PT, skip_runtime_bounds_check_because=
                                      "ranges hold edge tiles up to the first of padding only, far from the table's end")

        def load_ranges(e, group):
            regs = [e.alloc_register(f"range{i}_{nc.next_id()}") for i in range(2 * GW)]
            e.reg_load(regs, ranges[0:1, bass.ds(group * 2 * GW, 2 * GW)])
            return regs

        with nc.Block() as block:
            @block.vector
            def _(dve):
                item = dve.alloc_register("item")
                dve.reg_mov(item, 0)
                with dve.Fori(0, TILES) as group:
                    regs = load_ranges(dve, group)
                    dve.tensor_copy(own_base[:, 0], base[:, bass.ds(group * GW, GW)]).then_inc(based, 1)
                    dve.wait_ge(based, group + 1)
                    dve.sem_inc(passed, 1)
                    for u in range(GW):
                        with dve.Fori(regs[2 * u], regs[2 * u + 1], PT) as t:
                            t = in_table(dve, t)
                            for i in range(PT):
                                n = dve.snap(dve.snap(item) + (i + 1))
                                dve.wait_ge(used, n)
                                dve.tensor_scalar(olo[:, i * P:(i + 1) * P], iota16[:, 0:P],
                                                  slo_t[:, bass.ds(t + i, 1)], None, ALU.is_equal)
                                dve.tensor_scalar(ohi[:, i * WC:(i + 1) * WC], iota16[:], key_t[:, bass.ds(t + i, 1)],
                                                  own_base[:, 0, u:u + 1], ALU.subtract, ALU.is_equal).then_inc(hot, 1)
                            dve.reg_add(item, item, PT)
                    dve.wait_ge(hot, dve.snap(item))
                    dve.sem_inc(passed, 1)

            @block.tensor
            def _(pe):
                pe.sem_inc(used, PT)
                item = pe.alloc_register("pitem")
                pe.reg_mov(item, 0)

                def windows(group, regs, half):
                    for u in range(half * HG, half * HG + HG):
                        b = u % 2
                        own = pe.snap(group * -1 + TILES)
                        pe.wait_ge(evac, group * GW + u + 1)
                        for h in range(2):
                            pe.matmul(pw[b][:, h, 0:WB], place[:, P - W - u * W:2 * P - W - u * W],
                                      spread[:, h, bass.ds(own, WB)], start=True, stop=False,
                                      skip_group_check=True)
                        with pe.Fori(regs[2 * u], regs[2 * u + 1], PT) as t:
                            for i in range(PT):
                                n = pe.snap(pe.snap(item) + (i + 1))
                                pe.wait_ge(hot, n)
                                for h in range(2):
                                    mm = pe.matmul(pw[b][:, h, 0:WB], olo[:, i * P:(i + 1) * P],
                                                   ohi[:, i * WC + h * WB:i * WC + h * WB + WB], start=False,
                                                   stop=False, skip_group_check=True)
                                mm.then_inc(used, 1)
                            pe.reg_add(item, item, PT)
                        pe.matmul(pw[b][:, 1, 0:1], zeros16[:, 0:P], zeros16[:, 0:1], start=False, stop=True,
                                  skip_group_check=True).then_inc(win, 1)

                def start_degrees(b):
                    built, summed = pe.snap(b * BW + BW + 2), pe.snap(b + 2)
                    pe.wait_ge(evac, built)
                    pe.wait_ge(degout, summed)
                    pe.matmul(pd[:, 0:BLK], zeros16[:, 0:P], zeros16[:], start=True, stop=False, skip_group_check=True)

                def degrees(par, k0):
                    for k in range(KC):
                        mm = pe.matmul(pd[:, 0:BLK], ones16[:], blocks16[par][:, bass.ds(k0 * KC + k, 1), :]
                                       .rearrange("p o d -> p (o d)"), start=False, stop=False, skip_group_check=True)
                    mm.then_inc(deg, 1)

                pe.wait_ge(e_zero, 1)
                pe.matmul(pd[:, 0:BLK], zeros16[:, 0:P], zeros16[:], start=True, stop=False, skip_group_check=True)
                with pe.Fori(0, PAIRS) as pair:
                    with pe.Fori(0, KC // 2) as g:
                        group = pe.snap(pair * KC + g)
                        regs = load_ranges(pe, group)
                        for half in range(2):
                            windows(group, regs, half)
                            degrees(1, g * 2 + half)
                    group = pe.snap(pair * KC + KC // 2)
                    regs = load_ranges(pe, group)
                    windows(group, regs, 0)
                    degrees(1, KC - 1)
                    start_degrees(pe.snap(pair * 2))
                    windows(group, regs, 1)
                    degrees(0, 0)
                    with pe.Fori(0, KC // 2) as g:
                        group = pe.snap(pair * KC + KC // 2 + 1 + g)
                        regs = load_ranges(pe, group)
                        for half in range(2):
                            windows(group, regs, half)
                            degrees(0, g * 2 + 1 + half)
                    start_degrees(pe.snap(pair * 2 + 1))
                with pe.Fori(0, CHUNKS) as q:
                    degrees(1, q)

            @block.scalar
            def _(act):
                act.sem_inc(evac, 2)
                act.sem_inc(degout, 1)
                act.preload_act_table(ACT.Identity)
                with act.Fori(0, PAIRS) as pair:
                    for par in range(2):
                        b = act.snap(pair * 2 + par)
                        act.wait_ge(free, b + 1)
                        act.sem_inc(passed, 1)
                        with act.Fori(0, BW // 2) as q:
                            for u in range(2):
                                act.wait_ge(win, b * BW + q * 2 + u + 1)
                                act.activation(
                                    blocks16[par][:, :, bass.ds(q * 2 * W + u * W, W)]
                                    .rearrange("p s (h d) -> p s h d", h=2),
                                    pw[u][:, :, 0:WB].rearrange("p h (d s) -> p s h d", s=TILES), ACT.Copy,
                                    scale=ASCALE).then_inc(evac, 1)
                        act.wait_ge(deg, b * CHUNKS + CHUNKS)
                        act.activation(dinv_all[:, bass.ds(b * BLK, BLK)], pd[:, 0:BLK], ACT.Copy,
                                       scale=1.0 / ASCALE).then_inc(degout, 1)
                act.wait_ge(deg, BLOCKS * CHUNKS + CHUNKS)
                act.activation(dinv_all[:, NP:NP + BLK], pd[:, 0:BLK], ACT.Copy, scale=1.0 / ASCALE)

            @block.sync
            def _(sp):
                sp.sem_inc(free, 2)
                with sp.Fori(0, PAIRS) as pair:
                    for par in range(2):
                        b = sp.snap(pair * 2 + par)
                        sp.wait_ge(evac, sp.snap(b * BW + BW + 2))
                        sp.sem_inc(passed, 1)
                        sp.dma_start(adj[bass.ds(b, 1)].rearrange("o p n -> (o p) n"),
                                     blocks16[par].rearrange("p s d -> p (s d)")).then_inc(stored, 16)
                        sp.wait_ge(stored, sp.snap(b * 16 + 16))
                        sp.sem_inc(free, 1)

        r_step, r_root = sem("r_step"), sem("r_root")
        with nc.Block() as block:
            @block.scalar
            def _(act):
                act.activation(dinv_row, dinv_row, ACT.Sqrt).then_inc(r_root, 1)

            @block.vector
            def _(dve):
                dve.wait_ge(r_root, 1)
                prod = feat[:].rearrange("p f n -> p (f n)")[:, 0:NP].rearrange("p (t c) -> p t c", t=TILES)
                dve.reciprocal(dinv_row, dinv_row).then_inc(r_step, 1)
                dve.wait_ge(r_step, 1)
                dve.tensor_tensor(prod, dinv_row.rearrange("p (t c) -> p t c", t=TILES),
                                  ident[:].unsqueeze(1).broadcast_to([P, TILES, P]), ALU.mult).then_inc(r_step, 1)
                dve.wait_ge(r_step, 2)
                dve.tensor_reduce(dinv_col[:], prod, AX.X, ALU.add)


def load_and_norm(nc, sem, x, nodes, feat, ident, mean, rstd, stage):
    with ExitStack() as ctx:
        stats = ctx.enter_context(nc.sbuf_tensor("stats", [P, TILES, BN], F32))
        aggr = ctx.enter_context(nc.sbuf_tensor("aggr", [P, TILES, 2], F32))
        tp = [ctx.enter_context(nc.psum_tensor(f"xt{i}", [P, D], F32)) for i in range(2)]
        l_pad, l_x, l_st, l_root, l_dve, l_n, l_t, l_o = (sem(n) for n in ("l_pad", "l_x", "l_st", "l_root", "l_dve", "l_n", "l_t", "l_o"))
        full = (TILES - 1) * P
        with nc.Block() as block:
            @block.sync
            def _(sp):
                sp.dma_start(nodes[:, 0:TILES - 1, :], x[0:full, :].rearrange("(t p) d -> p t d", p=P)).then_inc(l_x, 16)
                sp.wait_ge(l_pad, 1)
                sp.dma_start(nodes[0:LAST, TILES - 1, :], x[full:N, :]).then_inc(l_x, 16)

            @block.vector
            def _(dve):
                dve.memset(nodes[:, TILES - 1, :], 0.0).then_inc(l_pad, 1)
                dve.wait_ge(l_x, 32)
                with dve.Fori(0, TILES) as t:
                    dve.bn_stats(stats[:, bass.ds(t, 1), :].rearrange("p o s -> p (o s)"),
                                 nodes[:, bass.ds(t, 1), :].rearrange("p o d -> p (o d)")).then_inc(l_st, 1)
                dve.wait_ge(l_st, TILES)
                for t in range(TILES):
                    dve.bn_aggr(aggr[:, t, :], stats[:, t, :]).then_inc(l_st, 1)
                dve.wait_ge(l_st, 2 * TILES)
                dve.tensor_copy(mean[:], aggr[:, :, 0]).then_inc(l_dve, 1)
                dve.tensor_scalar(rstd[:], aggr[:, :, 1], EPS, None, ALU.add).then_inc(l_dve, 1)
                dve.wait_ge(l_root, 1)
                dve.reciprocal(rstd[:], rstd[:]).then_inc(l_dve, 1)
                dve.wait_ge(l_dve, 3)

                def norm(t, u):
                    dve.wait_ge(l_t, t + 1)
                    dve.tensor_scalar(stage[:, u], nodes[:, bass.ds(t, 1), :].rearrange("p o d -> p (o d)"),
                                      mean[:, bass.ds(t, 1)], rstd[:, bass.ds(t, 1)], ALU.subtract,
                                      ALU.mult).then_inc(l_n, 1)

                with dve.Fori(0, TILES // 2) as q:
                    for u in range(2):
                        norm(dve.snap(q * 2 + u), u)
                norm(TILES - 1, 0)

            @block.tensor
            def _(pe):
                pe.sem_inc(l_t, 2)

                def turn(t, u):
                    pe.wait_ge(l_n, t + 1)
                    pe.wait_ge(l_o, t + 1)
                    for f in range(HALVES):
                        mm = pe.transpose(tp[u][:, f * P:(f + 1) * P], stage[:, u, f * P:(f + 1) * P], ident[:])
                    mm.then_inc(l_t, 1)

                with pe.Fori(0, TILES // 2) as q:
                    for u in range(2):
                        turn(pe.snap(q * 2 + u), u)
                turn(TILES - 1, 0)

            @block.scalar
            def _(act):
                act.sem_inc(l_o, 2)
                act.wait_ge(l_dve, 2)
                act.activation(rstd[:], rstd[:], ACT.Sqrt).then_inc(l_root, 1)
                act.preload_act_table(ACT.Identity)

                def put(t, u):
                    act.wait_ge(l_t, t + 3)
                    act.activation(feat[:, :, bass.ds(t * P, P)], tp[u][:].rearrange("p (f n) -> p f n", f=HALVES),
                                   ACT.Copy).then_inc(l_o, 1)

                with act.Fori(0, TILES // 2) as q:
                    for u in range(2):
                        put(act.snap(q * 2 + u), u)
                put(TILES - 1, 0)


def layer(nc, sem, l, adj, feat, hh, chunk, dinv_row, dinv_col, gw_sb, gb_sb, small, smalli, stage):
    relu = l < 2
    with ExitStack() as ctx:
        hp = [ctx.enter_context(nc.psum_tensor(f"hp{l}_{i}", [P, D], F32)) for i in range(2)]
        g_st, g_mm, g_h = (sem(f"{n}{l}") for n in ("g_staged", "g_product", "g_h"))
        m_v, m_p, m_s, m_hi, m_lo = (sem(f"{n}{l}") for n in ("m_max", "m_all", "m_scale", "m_hi", "m_lo"))
        pmax, amax, scale, unscale = (small[:, i:i + 1] for i in range(4))
        expo = smalli[:, 0:1]
        with nc.Block() as block:
            @block.scalar
            def _(act):
                act.preload_act_table(ACT.Identity)

                def put(t, u):
                    act.wait_ge(g_mm, t + 1)
                    act.activation(stage[:, u].rearrange("p (f n) -> p f n", f=HALVES), feat[:, :, bass.ds(t * P, P)],
                                   ACT.Copy).then_inc(g_st, 1)

                with act.Fori(0, TILES // 2) as q:
                    for u in range(2):
                        put(act.snap(q * 2 + u), u)
                put(TILES - 1, 0)
                act.wait_ge(m_v, 5)
                for q in range(CHUNKS):
                    s = slice(q * NP // CHUNKS, (q + 1) * NP // CHUNKS)
                    act.activation(hh[:, 0, :, s], feat[:, :, s], ACT.Copy, scale=scale).then_inc(m_hi, 1)

            @block.tensor
            def _(pe):
                pe.sem_inc(g_mm, 2)

                def product(t, u):
                    pe.wait_ge(g_st, t + 1)
                    pe.wait_ge(g_h, t + 1)
                    for f in range(HALVES):
                        mm = pe.matmul(hp[u][:], stage[:, u, f * P:(f + 1) * P], gw_sb[:, l, f, :],
                                       start=f == 0, stop=f == HALVES - 1)
                    mm.then_inc(g_mm, 1)

                with pe.Fori(0, TILES // 2) as q:
                    for u in range(2):
                        product(pe.snap(q * 2 + u), u)
                product(TILES - 1, 0)

            @block.vector
            def _(dve):
                dve.sem_inc(g_h, 2)

                def put(t, u):
                    dve.wait_ge(g_mm, t + 3)
                    dve.tensor_scalar(feat[:, :, bass.ds(t * P, P)], hp[u][:].rearrange("p (f n) -> p f n", f=HALVES),
                                      dinv_col[:, bass.ds(t, 1)], None, ALU.mult).then_inc(g_h, 1)

                with dve.Fori(0, TILES // 2) as q:
                    for u in range(2):
                        put(dve.snap(q * 2 + u), u)
                put(TILES - 1, 0)
                dve.wait_ge(g_h, TILES + 2)
                dve.tensor_reduce(pmax, feat[:].rearrange("p f n -> p (f n)"), AX.X, ALU.max,
                                  apply_absolute_value=True).then_inc(m_v, 1)
                dve.wait_ge(m_p, 1)
                dve.tensor_scalar(amax, amax, 2.0 ** -90, None, ALU.max).then_inc(m_v, 1)
                dve.wait_ge(m_v, 2)
                dve.tensor_scalar(expo, amax.bitcast(I32), 0x7F800000, None, ALU.bitwise_and).then_inc(m_v, 1)
                dve.wait_ge(m_v, 3)
                dve.tensor_scalar(scale.bitcast(I32), expo, -1.0, float((127 + 127 + 13) << 23), ALU.mult,
                                  ALU.add).then_inc(m_v, 1)
                dve.tensor_scalar(unscale, expo.bitcast(F32), 2.0 ** -13 / ASCALE, None, ALU.mult).then_inc(m_v, 1)
                dve.wait_ge(m_v, 5)
                for q in range(CHUNKS):
                    dve.wait_ge(m_hi, q + 1)
                    s = slice(q * NP // CHUNKS, (q + 1) * NP // CHUNKS)
                    dve.scalar_tensor_tensor(hh[:, 1, :, s], feat[:, :, s], scale, hh[:, 0, :, s], ALU.mult,
                                             ALU.subtract).then_inc(m_lo, 1)

            @block.gpsimd
            def _(pool):
                pool.wait_ge(m_v, 1)
                pool.partition_all_reduce(amax, pmax, P, RED.max).then_inc(m_p, 1)

    with ExitStack() as ctx:
        ap = [[ctx.enter_context(nc.psum_tensor(f"ap{l}_{i}{f}", [P, 512], F32)) for f in range(HALVES)] for i in range(2)]
        tmp = ctx.enter_context(nc.sbuf_tensor(f"tmp{l}", [P, 2, HALVES, BLK], F32))
        a_in = [sem(f"a_in{l}_{k}") for k in range(CHUNKS)]
        a_used, a_passed, a_scaled, a_out = (sem(f"{n}{l}") for n in ("a_used", "a_passed", "a_scaled", "a_out"))
        unscale = small[:, 3:4]
        with nc.Block() as block:
            @block.sync
            def _(sp):
                def fetch(b):
                    for k in range(CHUNKS):
                        if not isinstance(b, int):
                            sp.wait_ge(a_used, sp.snap(b * CHUNKS - CHUNKS + k + 1, min_val=1))
                            sp.sem_inc(a_passed, 1)
                        sp.dma_start(chunk[:, k].rearrange("p k d -> p (k d)"),
                                     adj[bass.ds(b, 1), :, k * KC * BLK:(k + 1) * KC * BLK]
                                     .rearrange("o p n -> (o p) n")).then_inc(a_in[k], 16)

                fetch(0)
                with sp.Fori(1, BLOCKS) as b:
                    fetch(b)

            @block.tensor
            def _(pe):
                with pe.Fori(0, PAIRS) as pair:
                    for par in range(2):
                        b = pe.snap(pair * 2 + par)
                        pe.wait_ge(a_scaled, b * HALVES + 1)
                        pe.wait_ge(a_scaled, b * HALVES + 2)
                        for k in range(TILES):
                            if k % KC == 0:
                                pe.wait_ge(a_in[k // KC], b * 16 + 16)
                            for f in range(HALVES):
                                for q in range(2):
                                    mm = pe.matmul(ap[par][f][:, 0:BLK], hh[:, q, f, k * P:(k + 1) * P],
                                                   chunk[:, k // KC, k % KC, :], start=(k == 0 and q == 0),
                                                   stop=(k == TILES - 1 and q == 1))
                            if k % KC == KC - 1:
                                mm.then_inc(a_used, 1)

            @block.vector
            def _(dve):
                dve.sem_inc(a_scaled, 2 * HALVES)

                with dve.Fori(0, PAIRS) as pair:
                    for par in range(2):
                        b = dve.snap(pair * 2 + par)
                        dve.wait_ge(a_used, b * CHUNKS + CHUNKS)
                        for f in range(HALVES):
                            dve.wait_ge(a_out, b * HALVES + f + 1)
                            dve.tensor_tensor(tmp[:, par, f], ap[par][f][:, 0:BLK], dinv_row[:, bass.ds(b * BLK, BLK)],
                                              ALU.mult).then_inc(a_scaled, 1)

            @block.scalar
            def _(act):
                act.sem_inc(a_out, 2 * HALVES)
                act.preload_act_table(ACT.Identity)
                with act.Fori(0, PAIRS) as pair:
                    for par in range(2):
                        b = act.snap(pair * 2 + par)
                        for f in range(HALVES):
                            act.wait_ge(a_scaled, b * HALVES + f + 1 + 2 * HALVES)
                            act.activation(feat[:, f, bass.ds(b * BLK, BLK)], tmp[:, par, f],
                                           ACT.Relu if relu else ACT.Identity, bias=gb_sb[:, l, f:f + 1],
                                           scale=unscale).then_inc(a_out, 1)


def finish(nc, sem, x, nodes, feat, big_b, dinv_row, ident, ones, mean, rstd, stage, small, route_row,
           wr, br, w1, b1, w2, b2, out):
    full = (TILES - 1) * P
    with ExitStack() as ctx:
        def sb(name, shape, dt):
            return ctx.enter_context(nc.sbuf_tensor(name, shape, dt))

        free = big_b[:].bitcast(F32)
        w1_sb = sb("w1_sb", [P, HALVES, HID], F32)
        w2_sb = free[:, 0:HM * D].rearrange("p (m n) -> p m n", m=HM)
        hid_flat = free[:, HM * D:HM * D + HM * 7 * P]
        hid = hid_flat.rearrange("p (m n) -> p m n", m=HM)
        stats = sb("fstats", [P, TILES, BN], F32)
        aggr = sb("faggr", [P, TILES, 2], F32)
        wr_b = sb("wr_b", [P, D], F32)
        b2_b = sb("b2_b", [P, D], F32)
        b1_sb = sb("b1_sb", [P, HM], F32)
        br_b = sb("br_b", [P, 1], F32)
        route = sb("route", [P, TILES], F32)
        turned = sb("turned", [TILES, P], F32)
        xn = sb("xn", [P, 2, D], F32)
        junk = sb("junk", [P, D], F32)
        psz = [ctx.enter_context(nc.psum_tensor(f"fp{i}", [P, 512], F32)) for i in range(8)]
        f_w, f_pad, f_x, f_g, f_t, f_x1, f_st, f_v, f_root = (sem(n) for n in ("f_w", "f_pad", "f_x", "f_g", "f_t", "f_x1", "f_st", "f_v", "f_root"))
        with nc.Block() as block:
            @block.sync
            def _(sp):
                sp.dma_start(nodes[:, 0:TILES - 1, :], x[0:full, :].rearrange("(t p) d -> p t d", p=P)).then_inc(f_x, 16)
                sp.dma_start(w1_sb[:], w1.rearrange("(k p) n -> p k n", p=P)).then_inc(f_w, 16)
                sp.dma_start(w2_sb, w2.rearrange("(m p) n -> p m n", p=P)).then_inc(f_w, 16)
                with nc.allow_non_contiguous_dma(reason="small vectors"):
                    sp.dma_start(b1_sb[:], b1.rearrange("(m p) -> p m", p=P)).then_inc(f_w, 16)
                    sp.dma_start(wr_b[:], wr.rearrange("d o -> o d").broadcast_to([P, D])).then_inc(f_w, 16)
                sp.dma_start(b2_b[:], b2.rearrange("(o d) -> o d", o=1).broadcast_to([P, D])).then_inc(f_w, 16)
                sp.dma_start(br_b[:], br.rearrange("(o d) -> o d", o=1).broadcast_to([P, 1])).then_inc(f_w, 16)
                sp.wait_ge(f_pad, 1)
                sp.dma_start(nodes[0:LAST, TILES - 1, :], x[full:N, :]).then_inc(f_x, 16)
                sp.wait_ge(f_w, 96)

            @block.scalar
            def _(act):
                act.preload_act_table(ACT.Identity)
                act.sem_inc(f_t, 2)

                def put(t, u):
                    act.wait_ge(f_t, t + 1)
                    act.activation(stage[:, u].rearrange("p (f n) -> p f n", f=HALVES), feat[:, :, bass.ds(t * P, P)],
                                   ACT.Copy).then_inc(f_g, 1)

                with act.Fori(0, TILES // 2) as q:
                    for u in range(2):
                        put(act.snap(q * 2 + u), u)
                put(TILES - 1, 0)
                act.wait_ge(f_v, 1)
                act.activation(rstd[:], rstd[:], ACT.Sqrt).then_inc(f_root, 1)

            @block.tensor
            def _(pe):
                pe.sem_inc(f_x1, 2)

                def turn(t, u):
                    pe.wait_ge(f_g, t + 1)
                    pe.wait_ge(f_x1, t + 1)
                    for f in range(HALVES):
                        mm = pe.transpose(psz[u][:, f * P:(f + 1) * P], stage[:, u, f * P:(f + 1) * P], ident[:])
                    mm.then_inc(f_t, 1)

                with pe.Fori(0, TILES // 2) as q:
                    for u in range(2):
                        turn(pe.snap(q * 2 + u), u)
                turn(TILES - 1, 0)

            @block.vector
            def _(dve):
                dve.memset(nodes[:, TILES - 1, :], 0.0).then_inc(f_pad, 1)
                dve.wait_ge(f_x, 32)

                def put(t, u):
                    tile = nodes[:, bass.ds(t, 1), :].rearrange("p o d -> p (o d)")
                    dve.wait_ge(f_t, t + 3)
                    dve.tensor_tensor(tile, tile, psz[u][:, 0:D], ALU.add).then_inc(f_x1, 1)

                with dve.Fori(0, TILES // 2) as q:
                    for u in range(2):
                        put(dve.snap(q * 2 + u), u)
                put(TILES - 1, 0)
                dve.wait_ge(f_x1, TILES + 2)
                with dve.Fori(0, TILES) as t:
                    dve.bn_stats(stats[:, bass.ds(t, 1), :].rearrange("p o s -> p (o s)"),
                                 nodes[:, bass.ds(t, 1), :].rearrange("p o d -> p (o d)")).then_inc(f_st, 1)
                dve.wait_ge(f_st, TILES)
                for t in range(TILES):
                    dve.bn_aggr(aggr[:, t, :], stats[:, t, :]).then_inc(f_st, 1)
                dve.wait_ge(f_st, 2 * TILES)
                dve.tensor_copy(mean[:], aggr[:, :, 0])
                dve.tensor_scalar(rstd[:], aggr[:, :, 1], EPS, None, ALU.add).then_inc(f_v, 1)
                dve.wait_ge(f_root, 1)
                dve.reciprocal(rstd[:], rstd[:])

        n_x, n_t, n_o, n_r, n_b = (sem(n) for n in ("n_x", "n_t", "n_o", "n_r", "n_b"))
        with nc.Block() as block:
            @block.vector
            def _(dve):
                def one(t, u):
                    tile = nodes[:, bass.ds(t, 1), :].rearrange("p o d -> p (o d)")
                    dve.wait_ge(n_t, t + 1)
                    dve.tensor_scalar(xn[:, u], tile, mean[:, bass.ds(t, 1)], rstd[:, bass.ds(t, 1)], ALU.subtract,
                                      ALU.mult).then_inc(n_x, 1)
                    dve.wait_ge(n_x, t + 1)
                    dve.scalar_tensor_tensor(junk[:], xn[:, u], 1.0, wr_b[:], ALU.mult, ALU.mult,
                                             accum_out=route[:, bass.ds(t, 1)]).then_inc(n_r, 1)
                    dve.tensor_tensor(tile, tile, xn[:, u], ALU.add).then_inc(n_b, 1)
                    dve.wait_ge(n_r, t + 1)

                with dve.Fori(0, TILES // 2) as q:
                    for u in range(2):
                        one(dve.snap(q * 2 + u), u)
                one(TILES - 1, 0)
                dve.tensor_scalar(route[:], route[:], br_b[:], None, ALU.add).then_inc(n_r, 1)

            @block.tensor
            def _(pe):
                pe.sem_inc(n_t, 2)

                def turn(t, u):
                    pe.wait_ge(n_x, t + 1)
                    pe.wait_ge(n_o, t + 1)
                    pe.wait_ge(n_b, t + 1)
                    pe.wait_ge(n_r, t + 1)
                    for f in range(HALVES):
                        mm = pe.transpose(psz[u][:, f * P:(f + 1) * P], xn[:, u, f * P:(f + 1) * P], ident[:])
                    mm.then_inc(n_t, 1)

                with pe.Fori(0, TILES // 2) as q:
                    for u in range(2):
                        turn(pe.snap(q * 2 + u), u)
                turn(TILES - 1, 0)
                pe.wait_ge(n_r, TILES + 1)
                pe.transpose(psz[2][0:TILES, 0:P], route[:], ident[:]).then_inc(n_t, 1)

            n_w, n_d = sem("n_w"), sem("n_d")

            @block.scalar
            def _(act):
                act.sem_inc(n_o, 2)
                act.preload_act_table(ACT.Identity)

                def put(t, u):
                    act.wait_ge(n_t, t + 3)
                    act.activation(feat[:, :, bass.ds(t * P, P)], psz[u][:, 0:D].rearrange("p (f n) -> p f n", f=HALVES),
                                   ACT.Copy).then_inc(n_o, 1)

                with act.Fori(0, TILES // 2) as q:
                    for u in range(2):
                        put(act.snap(q * 2 + u), u)
                put(TILES - 1, 0)
                act.wait_ge(n_t, TILES + 3)
                act.activation(turned[:], psz[2][0:TILES, 0:P], ACT.Copy).then_inc(n_w, 1)

            @block.sync
            def _(sp):
                sp.wait_ge(n_w, 1)
                sp.dma_start(route_row, turned[:]).then_inc(n_d, 16)
                sp.wait_ge(n_d, 16)
                sp.dma_start(dinv_row, route_row.rearrange("(o t) p -> o (t p)", o=1).broadcast_to([P, NP])).then_inc(n_d, 16)
                sp.wait_ge(n_d, 32)

        more = sb("more", [P, TILES], F32)
        cand = sb("cand", [P, TILES], F32)
        tie = sb("tie", [P, TILES], F32)
        tri = sb("tri", [P, P], F32)
        before = sb("before", [P, TILES], F32)
        col = sb("col", [P, TILES], F32)
        ahead = sb("ahead", [P, TILES], F32)
        gate = sb("gate", [P, TILES], F32)
        idx_i = sb("idx_i", [P, TILES], I32)
        real = sb("real", [P, TILES], F32)
        zero49 = sb("zero49", [P, TILES], F32)
        best, allbest, room = (small[:, i:i + 1] for i in (8, 9, 10))
        s_c, s_v, s_p, s_m, s_g = (sem(n) for n in ("s_c", "s_v", "s_p", "s_m", "s_g"))
        h_mm, h_act, y_mm, y_out, o_dma = (sem(n) for n in ("h_mm", "h_act", "y_mm", "y_out", "o_dma"))
        y_t = sem("y_t")
        o_passed = sem("o_passed")
        rows = feat[:].rearrange("p f n -> p (f n)")
        work = hid_flat[:, 0:N // 2]
        with nc.Block() as block:
            @block.gpsimd
            def _(pool):
                pool.iota(idx_i[:], pattern=[[P, TILES]], base=0, channel_multiplier=1).then_inc(s_c, 1)
                pool.memset(tri[:], 1.0).then_inc(s_c, 1)
                pool.wait_ge(s_c, 2)
                pool.affine_select(out=tri[:], in_=tri[:], compare_op=ALU.is_gt, fill=0.0, base=0,
                                   pattern=[[1, P]], channel_multiplier=-1).then_inc(s_c, 1)
                pool.wait_ge(s_p, 1)
                pool.partition_all_reduce(allbest, best, P, RED.max).then_inc(s_p, 1)

            @block.vector
            def _(dve):
                n = [0]

                def done(ins):
                    n[0] += 1
                    ins.then_inc(s_v, 1)
                    dve.wait_ge(s_v, n[0])

                dve.wait_ge(s_c, 3)
                done(dve.tensor_scalar(real[:], idx_i[:], float(N), None, ALU.is_lt))
                done(dve.memset(zero49[:], 0.0))
                half = N // 2
                for t in range(TILES):
                    for h in range(2):
                        done(dve.tensor_scalar(work, dinv_row[:, h * half:(h + 1) * half], route[:, t:t + 1],
                                               0.0, ALU.is_gt, ALU.add, accum_out=(more, col)[h][:, t:t + 1]))
                done(dve.tensor_tensor(more[:], more[:], col[:], ALU.add))
                done(dve.scalar_tensor_tensor(cand[:], more[:], float(KEEP), real[:], ALU.is_lt, ALU.mult))
                done(dve.scalar_tensor_tensor(before[:], more[:], 1.0, cand[:], ALU.add, ALU.mult))
                dve.tensor_reduce(best, before[:], AX.X, ALU.max).then_inc(s_p, 1)
                dve.wait_ge(s_p, 2)
                done(dve.tensor_scalar(tie[:], before[:], allbest, None, ALU.is_equal))
                done(dve.tensor_scalar(room, allbest, -1.0, float(KEEP + 1), ALU.mult, ALU.add))
                dve.wait_ge(s_m, 1)
                done(dve.tensor_copy(col[:], psz[7][:, 64:64 + TILES]))
                done(dve.tensor_tensor_scan(ahead[:], col[:], zero49[:], 0.0, ALU.add, ALU.add))
                done(dve.tensor_tensor(ahead[:], ahead[:], col[:], ALU.subtract))
                done(dve.tensor_tensor(ahead[:], ahead[:], psz[7][:, 0:TILES], ALU.add))
                done(dve.scalar_tensor_tensor(ahead[:], ahead[:], room, tie[:], ALU.is_ge, ALU.mult))
                done(dve.tensor_tensor(cand[:], cand[:], ahead[:], ALU.subtract))
                done(dve.tensor_tensor(gate[:], cand[:], route[:], ALU.mult))

                with dve.Fori(0, 7) as c:
                    for i in range(7):
                        t = dve.snap(c * 7 + i)
                        tile = nodes[:, bass.ds(t, 1), :].rearrange("p o d -> p (o d)")
                        dve.wait_ge(y_mm, t + 2)
                        dve.tensor_tensor(xn[:, i % 2], psz[4 + i % 2][:, 0:D], b2_b[:], ALU.add).then_inc(y_t, 1)
                        dve.wait_ge(y_t, t + 2)
                        dve.scalar_tensor_tensor(tile, xn[:, i % 2], gate[:, bass.ds(t, 1)], tile, ALU.mult,
                                                 ALU.add).then_inc(y_out, 1)
                        dve.wait_ge(y_out, t + 1)

            @block.tensor
            def _(pe):
                pe.sem_inc(h_act, 4)
                pe.sem_inc(y_mm, 1)
                pe.sem_inc(y_t, 1)

                def ranks():
                    pe.wait_ge(s_v, 2 + 2 * TILES + 4)
                    pe.matmul(psz[7][:, 0:TILES], tri[:], tie[:], start=True, stop=True)
                    pe.matmul(psz[7][:, 64:64 + TILES], ones[:], tie[:], start=True, stop=True,
                              skip_group_check=True).then_inc(s_m, 1)

                def hidden(c, m):
                    for g in range(2):
                        r = (2 * m + g) % 4
                        pe.wait_ge(h_act, c * 2 * HM + 2 * m + g + 1)
                        for k in range(HALVES):
                            mm = pe.matmul(psz[r][:, 0:BLK], w1_sb[:, k, m * P:(m + 1) * P],
                                           feat[:, k, bass.ds(c * 2 * BLK + g * BLK, BLK)], start=k == 0,
                                           stop=k == HALVES - 1)
                        mm.then_inc(h_mm, 1)

                ranks()
                with pe.Fori(0, 7) as c:
                    for m in range(HM):
                        hidden(c, m)
                    pe.wait_ge(h_act, c * 2 * HM + 2 * HM + 4)
                    for i in range(7):
                        t = pe.snap(c * 7 + i)
                        pe.wait_ge(y_t, t + 1 if i == 0 else t)
                        for m in range(HM):
                            mm = pe.matmul(psz[4 + i % 2][:, 0:D], hid[:, m, i * P:(i + 1) * P], w2_sb[:, m, :],
                                           start=m == 0, stop=m == HM - 1)
                        mm.then_inc(y_mm, 1)

            @block.scalar
            def _(act):
                act.preload_act_table(ACT.Gelu_apprx_tanh)
                with act.Fori(0, 7) as c:
                    for m in range(HM):
                        for g in range(2):
                            r = (2 * m + g) % 4
                            act.wait_ge(h_mm, c * 2 * HM + 2 * m + g + 1)
                            if m == 0 and g == 0:
                                act.wait_ge(y_mm, c * 7 + 1)
                            act.activation(hid[:, m, g * BLK:(g + 1) * BLK], psz[r][:, 0:BLK], ACT.Gelu_apprx_tanh,
                                           bias=b1_sb[:, m:m + 1]).then_inc(h_act, 1)

            @block.sync
            def _(sp):
                with sp.Fori(0, 6) as c:
                    sp.wait_ge(y_out, c * 7 + 7)
                    sp.sem_inc(o_passed, 1)
                    sp.dma_start(out[bass.ds(c * 7 * P, 7 * P), :].rearrange("(t p) d -> p t d", p=P),
                                 nodes[:, bass.ds(c * 7, 7), :]).then_inc(o_dma, 16)
                sp.wait_ge(y_out, TILES)
                sp.dma_start(out[42 * P:48 * P, :].rearrange("(t p) d -> p t d", p=P), nodes[:, 42:48, :]).then_inc(o_dma, 16)
                sp.dma_start(out[48 * P:N, :], nodes[0:LAST, 48, :]).then_inc(o_dma, 16)
                sp.wait_ge(o_dma, 8 * 16)


_INS = ["x", "src", "dst", "L0_gnn_W1", "L0_gnn_b1", "L0_gnn_W2", "L0_gnn_b2", "L0_gnn_W3", "L0_gnn_b3",
        "L0_ffn_wr", "L0_ffn_br", "L0_ffn_w1", "L0_ffn_b1", "L0_ffn_w2", "L0_ffn_b2"]


def kernel(**inputs):
    import concourse.bacc as bacc
    from concourse.bass_utils import run_bass_kernel_spmd

    nc = bacc.Bacc("TRN2", target_bir_lowering=False, num_devices=1)
    arrays, a = {}, {}
    for name in _INS:
        array = np.ascontiguousarray(inputs[name])
        arrays[f"in_{name}"] = array
        a[name] = nc.dram_tensor(f"in_{name}", array.shape, mybir.dt.from_np(array.dtype), kind="ExternalInput").ap()
    out = nc.dram_tensor("out", (N, D), F32, kind="ExternalOutput").ap()
    build(nc, a["x"], a["src"], a["dst"], [a[f"L0_gnn_W{i}"] for i in (1, 2, 3)], [a[f"L0_gnn_b{i}"] for i in (1, 2, 3)],
          a["L0_ffn_wr"], a["L0_ffn_br"], a["L0_ffn_w1"], a["L0_ffn_b1"], a["L0_ffn_w2"], a["L0_ffn_b2"], out)
    r = run_bass_kernel_spmd(nc, [arrays], core_ids=[0])
    return r.results[0]["out"]
```

```python
from contextlib import ExitStack

import numpy as np
import concourse.bass as bass
from concourse import mybir

ALU = mybir.AluOpType
ACT = mybir.ActivationFunctionType
AX = mybir.AxisListType
F32 = mybir.dt.float32
F16 = mybir.dt.float16
I32 = mybir.dt.int32
RED = bass.bass_isa.ReduceOp

P = 128
D = 256
HALVES = D // P
N = 6250
TILES = -(-N // P)
NP = TILES * P
LAST = N - (TILES - 1) * P
E = 200000
EJ = 13
ET = P * EJ
EFULL = E // (EJ * P)
EREST = E - EFULL * EJ * P
W = 16
HW = W // 2
WB = HW * TILES
WC = 2 * WB
WINDOWS = NP // W
WP = 98
WG = WINDOWS // WP
BLK = 448
BLOCKS = NP // BLK
PAIRS = BLOCKS // 2
PAIR_TILES = 2 * BLK // P
MIDDLE = PAIR_TILES // 2
BW = BLK // W
GW = P // W
HG = GW // 2
PT = 4
TOGETHER = 2
SETS = 2
GROUP_KEYS = P * TILES
KC = 7
CHUNKS = TILES // KC
PAD = 8191
HID = 4 * D
HM = HID // P
KEEP = max(1, int(0.5 * N)) - 1
ASCALE = 0.25
EPS = 1e-5
BN = 6
EARLY = 4
LAG = 2
PIECES = (0, 1, 3, 7, 14, 21, 28, 35, 42)


def build(nc, x, src, dst, gw, gb, wr, br, w1, b1, w2, b2, out):
    ctx = ExitStack()
    with ctx:
        def sb(name, shape, dt):
            return ctx.enter_context(nc.sbuf_tensor(name, shape, dt))

        def sem(name):
            return ctx.enter_context(nc.semaphore(name))

        adj = nc.dram_tensor("adj", (BLOCKS, P, TILES * BLK), F16, kind="Internal").ap()
        tile_ends = nc.dram_tensor("tile_ends", (2, ET), F32, kind="Internal").ap()
        dinv_dram = nc.dram_tensor("dinv_dram", (TILES, P), F32, kind="Internal").ap()
        turned_xn = nc.dram_tensor("turned_xn", (PAIRS, P, 2 * BLK * HALVES), F32, kind="Internal").ap()

        big_a = sb("big_a", [P, TILES * D], F32)
        big_b = sb("big_b", [P, TILES * BLK], F16)
        feat_all = sb("feat", [P, LAG + TILES, D], F32)
        feat = feat_all[:, LAG:LAG + TILES, :]
        row_space = sb("row_space", [P, max(2 * ET + SETS * PT * (WC + P) // 2 + (PAIR_TILES + 2) * D,
                                            NP + 2 * BLK * HALVES + D)], F32)
        dinv_row = row_space[:, 0:NP]
        root_col = sb("root_col", [P, PAIR_TILES + TILES], F32)
        dinv_col = root_col[:, PAIR_TILES:PAIR_TILES + TILES]
        ident = sb("ident", [P, P], F32)
        ones = sb("ones", [P, P], F32)
        ones16 = sb("ones16", [P, P], F16)
        peaks = sb("peaks", [P, TILES], F32)
        route = sb("route", [P, TILES], F32)
        gw_sb = sb("gw_sb", [P, 3, HALVES, D], F32)
        gb_sb = sb("gb_sb", [P, 3, HALVES], F32)
        b2_b, b1_sb, br_b = sb("b2_b", [P, D], F32), sb("b1_sb", [P, HM], F32), sb("br_b", [P, 1], F32)
        wr_b = sb("wr_b", [P, D], F32)
        small = sb("small", [P, 16], F32)
        smalli = sb("smalli", [P, 8], I32)
        hh = big_a[:].bitcast(F16).rearrange("p (q n) -> p q n", q=2)
        blocks16 = [big_a[:].bitcast(F16)[:, 0:TILES * BLK].rearrange("p (s d) -> p s d", s=TILES),
                    big_b[:].rearrange("p (s d) -> p s d", s=TILES)]
        chunk = big_b[:].rearrange("p (c k d) -> p c k d", c=CHUNKS, k=KC)

        c_init, weights_in = sem("c_init"), sem("weights_in")

        with nc.Block() as block:
            @block.gpsimd
            def _(pool):
                pool.memset(ident[:], 0.0).then_inc(c_init, 1)
                pool.wait_ge(c_init, 1)
                pool.affine_select(out=ident[:], in_=ident[:], compare_op=ALU.not_equal, fill=1.0, base=0,
                                   pattern=[[-1, P]], channel_multiplier=1).then_inc(c_init, 1)

            @block.vector
            def _(dve):
                dve.memset(ones[:], 1.0)
                dve.memset(ones16[:], 1.0)

            @block.sync
            def _(sp):
                s = weights_in
                for l in range(3):
                    sp.dma_start(gw_sb[:, l], gw[l].rearrange("(k p) n -> p k n", p=P)).then_inc(s, 16)
                    with nc.allow_non_contiguous_dma(reason="a bias of 256 values"):
                        sp.dma_start(gb_sb[:, l], gb[l].rearrange("(k p) -> p k", p=P)).then_inc(s, 16)
                with nc.allow_non_contiguous_dma(reason="small vectors"):
                    sp.dma_start(b1_sb[:], b1.rearrange("(m p) -> p m", p=P)).then_inc(s, 16)
                    sp.dma_start(wr_b[:], wr.rearrange("d o -> o d").broadcast_to([P, D])).then_inc(s, 16)
                sp.dma_start(br_b[:], br.rearrange("(o d) -> o d", o=1).broadcast_to([P, 1])).then_inc(s, 16)
                sp.dma_start(b2_b[:], b2.rearrange("(o d) -> o d", o=1).broadcast_to([P, D])).then_inc(s, 16)

        build_adjacency(nc, sem, src, dst, x, adj, tile_ends, big_a, big_b, row_space, root_col, feat_all, ident,
                        ones, ones16, gw_sb, small, blocks16, weights_in)
        for l in range(3):
            layer(nc, sem, l, adj, feat, hh, chunk, row_space, dinv_row, dinv_col, gw_sb, gb_sb, small, smalli, peaks,
                  ident, dinv_dram, x, wr_b, route, turned_xn)
        finish(nc, sem, feat, big_a, big_b, ones, small, smalli, route, turned_xn, br_b, w1, b1_sb, w2, b2_b, out)


def build_adjacency(nc, sem, src, dst, x, adj, tile_ends, big_a, big_b, row_space, root_col, feat_all, ident,
                    ones, ones16, gw_sb, small, blocks16, weights_in):
    with ExitStack() as ctx:
        def sb(name, shape, dt):
            return ctx.enter_context(nc.sbuf_tensor(name, shape, dt))

        def ps(name, shape, dt):
            return ctx.enter_context(nc.psum_tensor(name, shape, dt))

        tmp = feat_all[:].rearrange("p t d -> p (t d)")
        dst_i = tmp[:, 0:ET].bitcast(I32)
        src_i = tmp[:, ET:2 * ET].bitcast(I32)
        dst_f = tmp[:, 2 * ET:3 * ET]
        key_r = tmp[:, 3 * ET:4 * ET]
        slo_r = tmp[:, 4 * ET:5 * ET]
        low_b = tmp[:, 5 * ET:6 * ET]
        high_b = tmp[:, 6 * ET:7 * ET]
        spare = lambda i: big_a[:, i * ET:(i + 1) * ET]
        scratch, iota_i, up, down = spare(0), spare(1).bitcast(I32), spare(2), spare(3)
        at = [0]

        def space(n):
            at[0] += n
            return row_space[:, at[0] - n:at[0]]

        key_t = space(ET)
        slo_t = space(ET)
        ohi = space(SETS * PT * WC // 2).bitcast(F16).rearrange("p (s n) -> p s n", s=SETS)
        olo = space(SETS * PT * P // 2).bitcast(F16).rearrange("p (s n) -> p s n", s=SETS)
        xs = space(PAIR_TILES * D).rearrange("p (t d) -> p t d", t=PAIR_TILES)
        normed = space(D)
        turned = space(D)
        root_pair = sb("root_pair", [P, 2 * BLK], F32)
        moments = sb("moments", [P, 4], F32)
        junk = sb("junk", [P, D], F32)
        total, minus_mean, spread_of, rstd = (moments[:, i:i + 1] for i in range(4))
        eps_sb = sb("eps", [P, 1], F32)
        absw = spare(5)[:, 0:HALVES * D].rearrange("p (f d) -> p f d", f=HALVES)
        iota16 = sb("iota16", [P, WC], F16)
        thr = sb("thr", [WP, 2, WG], F32)
        thr_i = sb("thr_i", [WP, 2, WG], I32)
        ends = sb("ends", [P, 2, EJ], F32)
        found = sb("found", [WP, 2, WG], F32)
        table = sb("table", [WP, WG, 2], I32)
        ranges = sb("ranges", [1, 2 * WINDOWS], I32)
        zeros16 = sb("zeros16", [P, BLK], F16)
        place = sb("place", [P, 2 * P - W], F16)
        spread = sb("spread", [P, 2, TILES + WB], F16)
        e_pad, e_rows, e_dve, e_pool, e_ends, e_rt, e_tr = (sem(n) for n in (
            "e_pad", "e_rows", "e_dve", "e_pool", "e_ends", "e_roundtrip", "e_transposed"))
        e_zero, e_colsum = sem("e_zero"), sem("e_colsum")
        e_bc, e_table, e_tload = sem("e_bc"), sem("e_table"), sem("e_tload")

        steps = {"all": 0}
        with ExitStack() as c2:
            tp = [c2.enter_context(nc.psum_tensor(f"tp{i}", [P, 4, P], F32)) for i in range(8)]
            with nc.Block() as block:
                @block.gpsimd
                def _(pool):
                    pool.iota(iota_i, pattern=[[1, ET]], base=0, channel_multiplier=0).then_inc(e_pool, 1)
                    pool.iota(thr_i[:, 0, :], pattern=[[W, WG]], base=0, channel_multiplier=W * WG).then_inc(e_pool, 1)
                    pool.iota(thr_i[:, 1, :], pattern=[[W, WG]], base=W, channel_multiplier=W * WG).then_inc(e_pool, 1)
                    pool.memset(place[:], 0.0).then_inc(e_pool, 1)
                    pool.memset(spread[:], 0.0).then_inc(e_pool, 1)
                    pool.memset(zeros16[:], 0.0).then_inc(e_pool, 1)
                    pool.memset(big_b[:].bitcast(F32), 0.0).then_inc(e_zero, 1)
                    pool.memset(xs, 0.0).then_inc(e_zero, 1)
                    pool.memset(normed, 0.0).then_inc(e_zero, 1)
                    pool.memset(root_pair[:], 0.0).then_inc(e_zero, 1)
                    pool.memset(eps_sb[:], EPS).then_inc(e_zero, 1)
                    pool.wait_ge(e_pool, 6)
                    pool.affine_select(out=place[0:W], in_=place[0:W], compare_op=ALU.not_equal, fill=1.0,
                                       base=P - W, pattern=[[-1, 2 * P - W]], channel_multiplier=1).then_inc(e_pool, 1)
                    for h in range(2):
                        pool.affine_select(out=spread[0:W, h], in_=spread[0:W, h], compare_op=ALU.not_equal, fill=1.0,
                                           base=TILES - HW * h * TILES, pattern=[[-1, TILES + WB]],
                                           channel_multiplier=TILES).then_inc(e_pool, 1)

                @block.sync
                def _(sp):
                    sp.wait_ge(e_pad, 2)
                    rows = lambda a: a[0:EFULL * EJ * P].rearrange("(p e) -> p e", p=EFULL)
                    rest = lambda a: a[EFULL * EJ * P:E].rearrange("(p e) -> p e", p=1)
                    sp.dma_start(dst_i[0:EFULL, :], rows(dst)).then_inc(e_rows, 16)
                    sp.dma_start(dst_i[EFULL:EFULL + 1, 0:EREST], rest(dst)).then_inc(e_rows, 16)
                    sp.dma_start(src_i[0:EFULL, :], rows(src)).then_inc(e_rows, 16)
                    sp.dma_start(src_i[EFULL:EFULL + 1, 0:EREST], rest(src)).then_inc(e_rows, 16)
                    sp.wait_ge(e_ends, 2)
                    sp.dma_start(tile_ends.rearrange("a (p j) -> p a j", p=P), ends[:]).then_inc(e_rt, 16)
                    sp.wait_ge(e_rt, 16)
                    sp.dma_start(low_b, tile_ends[0:1, :].broadcast_to([P, ET])).then_inc(e_bc, 16)
                    sp.dma_start(high_b, tile_ends[1:2, :].broadcast_to([P, ET])).then_inc(e_bc, 16)
                    sp.wait_ge(e_table, 1)
                    sp.dma_start(ranges[0:1, :], table[:].rearrange("p g c -> p (g c)")).then_inc(e_tload, 16)
                    sp.wait_ge(e_tload, 16)

                @block.vector
                def _(dve):
                    def done(ins, name=None):
                        steps["all"] += 1
                        if name:
                            steps[name] = steps["all"]
                        ins.then_inc(e_dve, 1)
                        dve.wait_ge(e_dve, steps["all"])

                    dve.memset(dst_i, PAD).then_inc(e_pad, 1)
                    dve.memset(src_i, 0).then_inc(e_pad, 1)
                    dve.wait_ge(e_pool, 3)
                    done(dve.tensor_copy(iota16[:], iota_i[:, 0:WC]))
                    done(dve.tensor_scalar(up, iota_i, 1.0, None, ALU.add))
                    done(dve.tensor_scalar(down, iota_i, -1.0, float(ET), ALU.mult, ALU.add))
                    done(dve.tensor_copy(thr[:], thr_i[:]))
                    dve.wait_ge(e_rows, 64)
                    done(dve.tensor_copy(dst_f, dst_i))
                    rows3 = dst_f.rearrange("p (j e) -> p j e", j=EJ)
                    dve.tensor_reduce(ends[:, 0, :], rows3, AX.X, ALU.min).then_inc(e_ends, 1)
                    dve.tensor_reduce(ends[:, 1, :], rows3, AX.X, ALU.max).then_inc(e_ends, 1)
                    done(dve.tensor_scalar(slo_r.bitcast(I32), src_i, 7, None, ALU.arith_shift_right))
                    done(dve.scalar_tensor_tensor(key_r, dst_f, float(TILES), slo_r.bitcast(I32), ALU.mult, ALU.add))
                    done(dve.tensor_scalar(key_r, key_r, float(GROUP_KEYS), None, ALU.add), "keys")
                    done(dve.tensor_scalar(dst_i, src_i, P - 1, None, ALU.bitwise_and))
                    done(dve.tensor_copy(slo_r, dst_i), "low sources")
                    for g in range(8):
                        dve.wait_ge(e_tr, g + 1)
                        r, j0, k = g // 4, 4 * (g % 4), min(4, EJ - 4 * (g % 4))
                        t = (key_t, slo_t)[r].rearrange("p (q j) -> p j q", j=EJ)
                        done(dve.tensor_copy(t[:, j0:j0 + k, :], tp[g][:, 0:k, :]))
                    dve.wait_ge(e_bc, 32)
                    for g in range(WG):
                        done(dve.scalar_tensor_tensor(scratch[0:WP], high_b[0:WP], thr[:, 0, g:g + 1], down[0:WP],
                                                      ALU.is_ge, ALU.mult))
                        done(dve.tensor_reduce(found[:, 0, g:g + 1], scratch[0:WP], AX.X, ALU.max))
                        done(dve.scalar_tensor_tensor(scratch[0:WP], low_b[0:WP], thr[:, 1, g:g + 1], up[0:WP],
                                                      ALU.is_lt, ALU.mult))
                        done(dve.tensor_reduce(found[:, 1, g:g + 1], scratch[0:WP], AX.X, ALU.max))
                    done(dve.tensor_scalar(found[:, 0, :], found[:, 0, :], -1.0, float(ET), ALU.mult, ALU.add))
                    done(dve.scalar_tensor_tensor(found[:, 1, :], found[:, 0, :], 1.0, found[:, 1, :], ALU.add, ALU.max))
                    done(dve.tensor_copy(table[:, :, 0], found[:, 0, :]))
                    dve.tensor_copy(table[:, :, 1], found[:, 1, :]).then_inc(e_table, 1)
                    dve.wait_ge(weights_in, 160)
                    done(dve.scalar_tensor_tensor(absw, gw_sb[:, 0], -1.0, gw_sb[:, 0], ALU.mult, ALU.max), "magnitudes")
                    dve.wait_ge(e_colsum, 1)
                    done(dve.tensor_reduce(small[:, 1:2], tp[0][:, 0:2, :].rearrange("p k n -> p (k n)"), AX.X, ALU.max))
                    done(dve.tensor_scalar(small[:, 1:2], small[:, 1:2], 1.01 * D ** 0.5, None, ALU.mult))

                @block.tensor
                def _(pe):
                    for g in range(8):
                        r, j0, k = g // 4, 4 * (g % 4), min(4, EJ - 4 * (g % 4))
                        rows = (key_r, slo_r)[r]
                        if g == 0:
                            pe.wait_ge(e_dve, steps["keys"])
                        if g == 4:
                            pe.wait_ge(e_dve, steps["low sources"])
                        for j in range(k):
                            mm = pe.transpose(tp[g][:, j, :], rows[:, (j0 + j) * P:(j0 + j + 1) * P], ident[:])
                        mm.then_inc(e_tr, 1)
                    pe.wait_ge(e_dve, steps["magnitudes"])
                    for f in range(HALVES):
                        mm = pe.matmul(tp[0][:, 0:2, :].rearrange("p k n -> p (k n)"), ones[:], absw[:, f], start=f == 0,
                                       stop=f == HALVES - 1)
                    mm.then_inc(e_colsum, 1)

        pw = [ps(f"pw{i}", [P, 2, 512], F32) for i in range(2)]
        pd, pc, px, ph = (ps(n, [P, 512], F32) for n in ("degrees", "roots_by_node", "turned_x", "product"))
        hot, used, win, evac, passed, deg, degout, free, based = (sem(n) for n in (
            "hot", "used", "win", "evac", "passed", "deg", "degout", "free", "based"))
        stored, x_early, x_late, x_tail, cols, cols_out = (sem(n) for n in (
            "stored", "x_early", "x_late", "x_tail", "cols", "cols_out"))
        moment, l_root, l_cent, l_rec, l_n, l_t, l_o, l_mm, l_h = (sem(n) for n in (
            "moment", "l_root", "l_centred", "l_reciprocal", "l_normed", "l_turned", "l_stationary", "l_product", "l_h"))

        def in_table(e, t):
            return nc.s_assert_within(t, 0, ET - PT, skip_runtime_bounds_check_because=
                                      "ranges hold edge tiles up to the first of padding only, far from the table's end")

        def load_ranges(e, group):
            regs = [e.alloc_register(f"range{i}_{nc.next_id()}") for i in range(2 * GW)]
            e.reg_load(regs, ranges[0:1, bass.ds(group * 2 * GW, 2 * GW)])
            return regs

        with nc.Block() as block:
            @block.vector
            def _(dve):
                item = dve.alloc_register("item")
                dve.reg_mov(item, 0)
                last = [dve.alloc_register(f"last{i}") for i in range(SETS)]
                for register in last:
                    dve.reg_mov(register, 0)
                with dve.Fori(0, TILES) as group:
                    regs = load_ranges(dve, group)
                    dve.tensor_scalar(key_t, key_t, float(GROUP_KEYS), None, ALU.subtract).then_inc(based, 1)
                    dve.wait_ge(based, group + 1)
                    dve.sem_inc(passed, 1)
                    for u in range(GW):
                        with dve.Fori(regs[2 * u], regs[2 * u + 1], PT) as t:
                            t = in_table(dve, t)
                            for i in range(0, PT, TOGETHER):
                                n = dve.snap(dve.snap(last[u % SETS]) + (i + TOGETHER))
                                dve.wait_ge(used, n)
                                dve.tensor_tensor(olo[:, u % SETS, i * P:(i + TOGETHER) * P]
                                                  .rearrange("p (i n) -> p i n", i=TOGETHER),
                                                  iota16[:, 0:P].unsqueeze(1).broadcast_to([P, TOGETHER, P]),
                                                  slo_t[:, bass.ds(t + i, TOGETHER)].unsqueeze(2).broadcast_to([P, TOGETHER, P]),
                                                  ALU.is_equal)
                                for j in range(i, i + TOGETHER):
                                    dve.tensor_scalar(ohi[:, u % SETS, j * WC:(j + 1) * WC], iota16[:],
                                                      key_t[:, bass.ds(t + j, 1)], float(-u * WC),
                                                      ALU.subtract, ALU.is_equal).then_inc(hot, 1)
                            dve.reg_add(item, item, PT)
                            dve.reg_mov(last[u % SETS], item)
                    dve.wait_ge(l_root, group + 1)
                    dve.reciprocal(rstd, rstd).then_inc(l_rec, 1)
                    dve.wait_ge(hot, dve.snap(item))
                    dve.sem_inc(passed, 1)

            @block.tensor
            def _(pe):
                pe.sem_inc(used, PT)
                item = pe.alloc_register("pitem")
                pe.reg_mov(item, 0)

                def windows(group, regs, half):
                    for u in range(half * HG, half * HG + HG):
                        b = u % 2
                        own = pe.snap(group * -1 + TILES)
                        pe.wait_ge(evac, group * GW + u + 1)
                        for h in range(2):
                            pe.matmul(pw[b][:, h, 0:WB], place[:, P - W - u * W:2 * P - W - u * W],
                                      spread[:, h, bass.ds(own, WB)], start=True, stop=False,
                                      skip_group_check=True)
                        with pe.Fori(regs[2 * u], regs[2 * u + 1], PT) as t:
                            for i in range(PT):
                                n = pe.snap(pe.snap(item) + (i + 1))
                                pe.wait_ge(hot, n)
                                for h in range(2):
                                    mm = pe.matmul(pw[b][:, h, 0:WB], olo[:, u % SETS, i * P:(i + 1) * P],
                                                   ohi[:, u % SETS, i * WC + h * WB:i * WC + h * WB + WB], start=False,
                                                   stop=False, skip_group_check=True)
                                mm.then_inc(used, 1)
                            pe.reg_add(item, item, PT)
                        pe.matmul(pw[b][:, 1, 0:1], zeros16[:, 0:P], zeros16[:, 0:1], start=False, stop=True,
                                  skip_group_check=True).then_inc(win, 1)

                def start_degrees(b):
                    built, summed = pe.snap(b * BW + BW + 2), pe.snap(b + 2)
                    pe.wait_ge(evac, built)
                    pe.wait_ge(degout, summed)
                    pe.matmul(pd[:, 0:BLK], zeros16[:, 0:P], zeros16[:], start=True, stop=False, skip_group_check=True)

                def by_node():
                    for i in range(PAIR_TILES):
                        mm = pe.matmul(pc[:, i:i + 1], root_pair[:, i * P:(i + 1) * P], ident[:, 0:1], start=True,
                                       stop=True, skip_group_check=True)
                    mm.then_inc(cols, 1)

                def turn(g):
                    pe.wait_ge(l_n, g + 1)
                    for f in range(HALVES):
                        mm = pe.transpose(px[:, f * P:(f + 1) * P], normed[:, f * P:(f + 1) * P], ident[:])
                    mm.then_inc(l_t, 1)

                def product(g):
                    pe.wait_ge(l_o, g + 1)
                    pe.wait_ge(l_h, g + 1)
                    for f in range(HALVES):
                        mm = pe.matmul(ph[:, 0:D], turned[:, f * P:(f + 1) * P], gw_sb[:, 0, f, :], start=f == 0,
                                       stop=f == HALVES - 1)
                    mm.then_inc(l_mm, 1)

                def degrees(par, k0):
                    for k in range(KC):
                        mm = pe.matmul(pd[:, 0:BLK], ones16[:], blocks16[par][:, bass.ds(k0 * KC + k, 1), :]
                                       .rearrange("p o d -> p (o d)"), start=False, stop=False, skip_group_check=True)
                    mm.then_inc(deg, 1)

                pe.wait_ge(e_zero, 1)
                pe.matmul(pd[:, 0:BLK], zeros16[:, 0:P], zeros16[:], start=True, stop=False, skip_group_check=True)
                pe.matmul(ph[:, 0:D], zeros16[:, 0:P], zeros16[:, 0:D], start=True, stop=True).then_inc(l_mm, 1)
                extra = (turn, product)
                with pe.Fori(0, PAIRS) as pair:
                    with pe.Fori(0, MIDDLE) as g:
                        group = pe.snap(pair * PAIR_TILES + g)
                        regs = load_ranges(pe, group)
                        for half in range(2):
                            windows(group, regs, half)
                            degrees(1, g * 2 + half)
                            extra[half](group)
                    group = pe.snap(pair * PAIR_TILES + MIDDLE)
                    regs = load_ranges(pe, group)
                    windows(group, regs, 0)
                    degrees(1, CHUNKS - 1)
                    turn(group)
                    start_degrees(pe.snap(pair * 2))
                    by_node()
                    windows(group, regs, 1)
                    degrees(0, 0)
                    product(group)
                    with pe.Fori(0, MIDDLE) as g:
                        group = pe.snap(pair * PAIR_TILES + MIDDLE + 1 + g)
                        regs = load_ranges(pe, group)
                        for half in range(2):
                            windows(group, regs, half)
                            degrees(0, g * 2 + 1 + half)
                            extra[half](group)
                    start_degrees(pe.snap(pair * 2 + 1))
                with pe.Fori(0, CHUNKS) as q:
                    degrees(1, q)
                turn(TILES)
                product(TILES)
                pe.wait_ge(degout, BLOCKS + 2)
                by_node()

            @block.scalar
            def _(act):
                act.sem_inc(evac, 2)
                act.sem_inc(degout, 1)
                act.sem_inc(l_n, 1)
                act.preload_act_table(ACT.Sqrt)

                def out_windows(par, column, window, between):
                    for u in range(HG):
                        act.wait_ge(win, window + (u + 1))
                        act.activation(blocks16[par][:, :, bass.ds(column + u * W, W)]
                                       .rearrange("p s (h d) -> p s h d", h=2),
                                       pw[u % 2][:, :, 0:WB].rearrange("p h (d s) -> p s h d", s=TILES), ACT.Copy,
                                       scale=ASCALE).then_inc(evac, 1)
                        between[u]()

                def out_product(g):
                    act.wait_ge(l_mm, g + 1)
                    act.activation(feat_all[:, bass.ds(g, 1), :].rearrange("p o d -> p (o d)"), ph[:, 0:D],
                                   ACT.Copy).then_inc(l_h, 1)

                def put(g):
                    act.wait_ge(l_t, g + 1)
                    act.activation(turned, px[:, 0:D], ACT.Copy).then_inc(l_o, 1)

                def tile_of_x(i):
                    return xs[:, bass.ds(i, 1), :].rearrange("p o d -> p (o d)")

                def sum_x(g, pair, i, part):
                    act.wait_ge((x_early, x_late)[part], pair * 16 + 16)
                    act.activation(junk[:], tile_of_x(i), ACT.Copy, accum_out=total).then_inc(moment, 1)

                def mean_x(g):
                    act.wait_ge(moment, g * 3 + 1)
                    act.activation(minus_mean, total, ACT.Copy, scale=-1.0 / D).then_inc(moment, 1)

                def squares_x(g, i):
                    act.wait_ge(moment, g * 3 + 2)
                    act.sem_inc(passed, 1)
                    act.activation(junk[:], tile_of_x(i), ACT.Square, bias=minus_mean,
                                   accum_out=spread_of).then_inc(moment, 1)

                def root_x(g):
                    act.wait_ge(moment, g * 3 + 3)
                    act.activation(rstd, spread_of, ACT.Sqrt, bias=eps_sb[:], scale=1.0 / D).then_inc(l_root, 1)

                def centre_x(i):
                    act.activation(normed, tile_of_x(i), ACT.Identity, bias=minus_mean).then_inc(l_cent, 1)

                def scale_x(g):
                    act.wait_ge(l_cent, g + 1)
                    act.wait_ge(l_rec, g + 1)
                    act.activation(normed, normed, ACT.Copy, scale=rstd).then_inc(l_n, 1)

                def half0(par, column, group, pair, i, part):
                    out_windows(par, column, group * GW, (
                        lambda: out_product(group), lambda: sum_x(group, pair, i, part), lambda: mean_x(group),
                        lambda: squares_x(group, i)))

                def half1(par, column, group, i):
                    out_windows(par, column, group * GW + HG, (
                        lambda: put(group), lambda: root_x(group), lambda: centre_x(i), lambda: scale_x(group)))

                def out_degrees(b, half):
                    act.wait_ge(deg, b * CHUNKS + CHUNKS)
                    act.activation(root_pair[:, half * BLK:(half + 1) * BLK], pd[:, 0:BLK], ACT.Sqrt,
                                   scale=1.0 / ASCALE).then_inc(degout, 1)

                def out_by_node(pair):
                    act.wait_ge(cols, pair + 1)
                    act.activation(root_col[:, bass.ds(pair * PAIR_TILES, PAIR_TILES)], pc[:, 0:PAIR_TILES],
                                   ACT.Copy).then_inc(cols_out, 1)

                def begin(b):
                    act.wait_ge(free, b + 1)
                    act.sem_inc(passed, 1)

                with act.Fori(0, PAIRS) as pair:
                    begin(act.snap(pair * 2))
                    with act.Fori(0, MIDDLE) as g:
                        group = act.snap(pair * PAIR_TILES + g)
                        half0(0, g * P, group, pair, g, 0)
                        half1(0, g * P + HG * W, group, g)
                    group = act.snap(pair * PAIR_TILES + MIDDLE)
                    half0(0, (MIDDLE) * P, group, pair, MIDDLE, 0)
                    out_degrees(act.snap(pair * 2), 1)
                    begin(act.snap(pair * 2 + 1))
                    half1(1, 0, group, MIDDLE)
                    out_by_node(pair)
                    with act.Fori(0, MIDDLE) as g:
                        group = act.snap(pair * PAIR_TILES + MIDDLE + 1 + g)
                        half0(1, g * P + HG * W, group, pair, g + (MIDDLE + 1), 1)
                        half1(1, g * P + 2 * HG * W, group, g + (MIDDLE + 1))
                    out_degrees(act.snap(pair * 2 + 1), 0)
                out_product(TILES)
                put(TILES)
                out_degrees(BLOCKS, 1)
                out_product(TILES + 1)
                out_by_node(PAIRS)

            @block.sync
            def _(sp):
                sp.sem_inc(free, 2)

                def load_x(pair, part):
                    i0, i1 = ((0, EARLY), (EARLY, PAIR_TILES))[part]
                    if not (isinstance(pair, int) and pair == 0):
                        sp.wait_ge(l_n, (pair - 1) * PAIR_TILES + (i1 + 1))
                        sp.sem_inc(passed, 1)
                    if isinstance(pair, int) and pair == PAIRS - 1 and part == 1:
                        i1 -= 1
                        sp.dma_start(xs[0:LAST, PAIR_TILES - 1, :], x[(TILES - 1) * P:N, :]).then_inc(x_tail, 16)
                        sp.wait_ge(x_tail, 16)
                    sp.dma_start(xs[:, i0:i1, :], x[bass.ds((pair * PAIR_TILES + i0) * P, (i1 - i0) * P), :]
                                 .rearrange("(t p) d -> p t d", p=P)).then_inc((x_early, x_late)[part], 16)

                def store(b, par):
                    sp.wait_ge(evac, b * BW + (BW + 2))
                    sp.sem_inc(passed, 1)
                    sp.dma_start(adj[bass.ds(b, 1)].rearrange("o p n -> (o p) n"),
                                 blocks16[par].rearrange("p s d -> p (s d)")).then_inc(stored, 16)

                def blocks_of(pair, following):
                    for par in range(2):
                        store(pair * 2 + par, par)
                        sp.wait_ge(stored, pair * 32 + (par * 16 + 16))
                        sp.sem_inc(free, 1)
                        if following is not None:
                            load_x(following, par)

                load_x(0, 0)
                load_x(0, 1)
                with sp.Fori(0, PAIRS - 2) as pair:
                    blocks_of(pair, sp.snap(pair + 1))
                blocks_of(PAIRS - 2, PAIRS - 1)
                blocks_of(PAIRS - 1, None)


def layer(nc, sem, l, adj, feat, hh, chunk, row_space, dinv_row, dinv_col, gw_sb, gb_sb, small, smalli, peaks,
          ident, dinv_dram, x, wr_b, route, turned_xn):
    last = l == 2
    with ExitStack() as ctx:
        def sb(name, shape):
            return ctx.enter_context(nc.sbuf_tensor(f"{name}{l}", shape, F32))

        def ps(name):
            return ctx.enter_context(nc.psum_tensor(f"{name}{l}", [P, 512], F32))

        ap = [[ps(f"agg{par}_{f}_") for f in range(HALVES)] for par in range(2)]
        hp = [ps(f"next{i}_") for i in range(2)]
        tmp = sb("tmp", [P, HALVES, BLK])
        fresh = sb("fresh", [P, HALVES, 2 * BLK])
        a_in = [sem(f"a_in{l}_{k}") for k in range(CHUNKS)]
        a_used, a_passed, a_scaled, a_out = (sem(f"{n}{l}") for n in ("a_used", "a_passed", "a_scaled", "a_out"))
        g_mm, g_h, g_peak = (sem(f"{n}{l}") for n in ("g_product", "g_h", "g_peak"))
        m_v, m_p, m_hi, m_lo = (sem(f"{n}{l}") for n in ("m_max", "m_all", "m_hi", "m_lo"))
        pmax, amax, scale, unscale = (small[:, i:i + 1] for i in range(4))
        expo = smalli[:, 0:1]
        h32 = feat.rearrange("p t d -> p (t d)")
        if l == 0:
            factor = sb("factor", [P, TILES])
            by_tile = ctx.enter_context(nc.sbuf_tensor("by_tile", [TILES, P], F32))
            d_row, d_col, d_turned = sem("d_row"), sem("d_col"), sem("d_turned")
        if last:
            xp = [ps(f"turn{i}_") for i in range(2)]
            junk = row_space[:, NP + 2 * BLK * HALVES:NP + 2 * BLK * HALVES + D]
            stats, aggr = sb("stats", [P, PAIR_TILES, BN]), sb("aggr", [P, PAIR_TILES, 2])
            rstd = sb("rstd", [P, PAIR_TILES])
            xn = sb("xn", [P, PAIR_TILES, D])
            xt = row_space[:, NP:NP + HALVES * PAIR_TILES * P].rearrange("p (f n) -> p f n", f=HALVES)
            x_in, x_pad, own, root, n_t, n_o, n_st, x_free = (sem(n) for n in (
                "x_in", "x_pad", "own", "root", "xn_turned", "xn_out", "xn_stored", "xt_free"))
        OWN = 4 * PAIR_TILES + 3

        with nc.Block() as block:
            @block.sync
            def _(sp):
                def fetch(b):
                    for k in range(CHUNKS):
                        if not isinstance(b, int) or b > 0:
                            sp.wait_ge(a_used, b * CHUNKS - CHUNKS + k + 1 if isinstance(b, int)
                                       else sp.snap(b * CHUNKS - CHUNKS + k + 1, min_val=1))
                            sp.sem_inc(a_passed, 1)
                        sp.dma_start(chunk[:, k].rearrange("p k d -> p (k d)"),
                                     adj[bass.ds(b, 1), :, k * KC * BLK:(k + 1) * KC * BLK]
                                     .rearrange("o p n -> (o p) n")).then_inc(a_in[k], 16)

                def store(p):
                    sp.wait_ge(n_o, p * PAIR_TILES + PAIR_TILES + 1)
                    sp.sem_inc(a_passed, 1)
                    sp.dma_start(turned_xn[bass.ds(p, 1)].rearrange("o p n -> (o p) n"),
                                 xt.rearrange("p f n -> p (f n)")).then_inc(n_st, 16)
                    sp.wait_ge(n_st, p * 16 + 16)
                    sp.sem_inc(x_free, 1)

                fetch(0)
                if l == 0:
                    sp.wait_ge(d_turned, 2)
                    sp.dma_start(dinv_dram, by_tile[:]).then_inc(d_row, 16)
                    sp.wait_ge(d_row, 16)
                    sp.dma_start(dinv_row, dinv_dram.rearrange("(o t) p -> o (t p)", o=1)
                                 .broadcast_to([P, NP])).then_inc(d_row, 16)
                if not last:
                    with sp.Fori(1, BLOCKS) as b:
                        fetch(b)
                else:
                    sp.sem_inc(x_free, 1)
                    sp.wait_ge(m_lo, len(PIECES))
                    full = (TILES - 1) * P
                    sp.dma_start(feat[:, 0:TILES - 1, :], x[0:full, :]
                                 .rearrange("(t p) d -> p t d", p=P)).then_inc(x_in, 16)
                    sp.wait_ge(x_pad, 1)
                    sp.dma_start(feat[0:LAST, TILES - 1, :], x[full:N, :]).then_inc(x_in, 16)
                    fetch(1)
                    fetch(2)
                    with sp.Fori(1, PAIRS - 1) as p:
                        fetch(sp.snap(p * 2 + 1))
                        fetch(sp.snap(p * 2 + 2))
                        store(sp.snap(p - 1))
                    fetch(BLOCKS - 1)
                    store(PAIRS - 2)
                    store(PAIRS - 1)

            @block.tensor
            def _(pe):
                pe.sem_inc(g_mm, 1)
                if last:
                    pe.sem_inc(n_t, 1)

                def aggregate(b, par, first=False):
                    pe.wait_ge(a_scaled, b * HALVES + 2)
                    for k in range(TILES):
                        if k % KC == 0:
                            pe.wait_ge(a_in[k // KC], b * 16 + 16)
                        if first and k in PIECES:
                            i = PIECES.index(k) + 1
                            pe.wait_ge(m_lo, (PIECES + (TILES,))[i] if l == 0 else i)
                        for f in range(HALVES):
                            for q in range(2):
                                mm = pe.matmul(ap[par][f][:, 0:BLK], hh[:, q, k * D + f * P:k * D + (f + 1) * P],
                                               chunk[:, k // KC, k % KC, :], start=(k == 0 and q == 0),
                                               stop=(k == TILES - 1 and q == 1))
                        if k % KC == KC - 1:
                            mm.then_inc(a_used, 1)

                def onward(p):
                    pe.wait_ge(a_out, p * 2 * HALVES + 2 * HALVES + HALVES)
                    for i in range(PAIR_TILES):
                        pe.wait_ge(g_h, p * PAIR_TILES + max(i - 1, 0) + 1)
                        if not last:
                            pe.wait_ge(g_peak, p * PAIR_TILES + max(i - 1, 0) + 1)
                        for f in range(HALVES):
                            tile = fresh[:, f, i * P:(i + 1) * P]
                            if last:
                                mm = pe.transpose(hp[i % 2][:, f * P:(f + 1) * P], tile, ident[:])
                            else:
                                mm = pe.matmul(hp[i % 2][:, 0:D], tile, gw_sb[:, l + 1, f, :], start=f == 0,
                                               stop=f == HALVES - 1)
                        mm.then_inc(g_mm, 1)

                def turn_xn(p):
                    pe.wait_ge(own, p * OWN + 3 * PAIR_TILES + 2 + 1)
                    for i in range(PAIR_TILES):
                        pe.wait_ge(n_o, p * PAIR_TILES + max(i - 1, 0) + 1)
                        for f in range(HALVES):
                            mm = pe.transpose(xp[i % 2][:, f * P:(f + 1) * P], xn[:, i, f * P:(f + 1) * P], ident[:])
                        mm.then_inc(n_t, 1)

                if l == 0:
                    pe.wait_ge(d_col, 1)
                    pe.transpose(hp[0][0:TILES, 0:P], dinv_col, ident[:]).then_inc(d_turned, 1)
                aggregate(0, 0, first=True)
                start = 0
                if last:
                    aggregate(1, 1)
                    aggregate(2, 0)
                    onward(0)
                    start = 1
                with pe.Fori(start, PAIRS - 1) as p:
                    aggregate(pe.snap(p * 2 + 1), 1)
                    if last:
                        turn_xn(pe.snap(p - 1))
                    aggregate(pe.snap(p * 2 + 2), 0)
                    onward(p)
                aggregate(BLOCKS - 1, 1)
                if last:
                    turn_xn(PAIRS - 2)
                onward(PAIRS - 1)
                if last:
                    turn_xn(PAIRS - 1)

            @block.vector
            def _(dve):
                dve.sem_inc(a_scaled, 2 * HALVES)
                dve.sem_inc(g_h, 1)
                dve.sem_inc(g_peak, 1)
                if l == 0:
                    dve.reciprocal(dinv_col, dinv_col).then_inc(d_col, 1)
                    dve.wait_ge(d_col, 1)
                if l == 0:
                    dve.sem_inc(m_v, 1)
                else:
                    dve.tensor_reduce(pmax, peaks[:], AX.X, ALU.max).then_inc(m_v, 1)
                    dve.wait_ge(m_p, 1)
                dve.tensor_scalar(amax, amax, 2.0 ** -90, None, ALU.max).then_inc(m_v, 1)
                dve.wait_ge(m_v, 2)
                dve.tensor_scalar(expo, amax.bitcast(I32), 0x7F800000, None, ALU.bitwise_and).then_inc(m_v, 1)
                dve.wait_ge(m_v, 3)
                dve.tensor_scalar(scale.bitcast(I32), expo, -1.0, float((127 + 127 + 13) << 23), ALU.mult,
                                  ALU.add).then_inc(m_v, 1)
                dve.tensor_scalar(unscale, expo.bitcast(F32), 2.0 ** -13 / ASCALE, None, ALU.mult).then_inc(m_v, 1)
                dve.wait_ge(m_v, 5)
                if l == 0:
                    dve.tensor_scalar(factor[:], dinv_col, scale, None, ALU.mult).then_inc(m_v, 1)
                    dve.wait_ge(m_v, 6)
                    with dve.Fori(0, PAIRS) as q:
                        for i in range(PAIR_TILES):
                            t = dve.snap(q * PAIR_TILES + i)
                            dve.wait_ge(m_hi, t + 1)
                            dve.scalar_tensor_tensor(hh[:, 1, bass.ds(t * D, D)], h32[:, bass.ds(t * D, D)],
                                                     factor[:, bass.ds(t, 1)], hh[:, 0, bass.ds(t * D, D)], ALU.mult,
                                                     ALU.subtract).then_inc(m_lo, 1)
                    dve.wait_ge(d_row, 32)
                else:
                    for i, t0 in enumerate(PIECES):
                        dve.wait_ge(m_hi, i + 1)
                        s = slice(t0 * D, (PIECES + (TILES,))[i + 1] * D)
                        dve.scalar_tensor_tensor(hh[:, 1, s], h32[:, s], scale, hh[:, 0, s], ALU.mult,
                                                 ALU.subtract).then_inc(m_lo, 1)
                if last:
                    dve.sem_inc(own, 1)
                    dve.wait_ge(m_lo, len(PIECES))
                    dve.memset(feat[:, TILES - 1, :], 0.0).then_inc(x_pad, 1)

                def scaled(b, par):
                    dve.wait_ge(a_used, b * CHUNKS + CHUNKS)
                    for f in range(HALVES):
                        dve.wait_ge(a_out, b * HALVES + f + 1)
                        dve.tensor_tensor(tmp[:, f], ap[par][f][:, 0:BLK], dinv_row[:, bass.ds(b * BLK, BLK)],
                                          ALU.mult).then_inc(a_scaled, 1)

                def next_h(p):
                    for i in range(PAIR_TILES):
                        t = p * PAIR_TILES + i if isinstance(p, int) else dve.snap(p * PAIR_TILES + i)
                        dve.wait_ge(g_mm, t + 2)
                        dve.tensor_reduce(peaks[:, bass.ds(t, 1)], hp[i % 2][:, 0:D], AX.X, ALU.max,
                                          apply_absolute_value=True).then_inc(g_peak, 1)
                        dve.tensor_scalar(feat[:, bass.ds(t, 1), :].rearrange("p o d -> p (o d)"), hp[i % 2][:, 0:D],
                                          dinv_col[:, bass.ds(t, 1)], None, ALU.mult).then_inc(g_h, 1)

                def next_x(p):
                    base = 1
                    for i in range(PAIR_TILES):
                        t = p * PAIR_TILES + i if isinstance(p, int) else dve.snap(p * PAIR_TILES + i)
                        tile = feat[:, bass.ds(t, 1), :].rearrange("p o d -> p (o d)")
                        dve.wait_ge(g_mm, t + 2)
                        dve.tensor_tensor(tile, tile, hp[i % 2][:, 0:D], ALU.add).then_inc(g_h, 1)
                    dve.wait_ge(g_h, p * PAIR_TILES + PAIR_TILES + 1)
                    dve.sem_inc(a_passed, 1)
                    for i in range(PAIR_TILES):
                        t = p * PAIR_TILES + i if isinstance(p, int) else dve.snap(p * PAIR_TILES + i)
                        dve.bn_stats(stats[:, i, :], feat[:, bass.ds(t, 1), :].rearrange("p o d -> p (o d)")).then_inc(own, 1)
                    dve.wait_ge(own, p * OWN + PAIR_TILES + base)
                    dve.sem_inc(a_passed, 1)
                    for i in range(PAIR_TILES):
                        dve.bn_aggr(aggr[:, i, :], stats[:, i, :]).then_inc(own, 1)
                    dve.wait_ge(own, p * OWN + 2 * PAIR_TILES + base)
                    dve.tensor_scalar(rstd[:], aggr[:, :, 1], EPS, None, ALU.add).then_inc(own, 1)
                    dve.wait_ge(root, p + 1)
                    dve.reciprocal(rstd[:], rstd[:]).then_inc(own, 1)
                    dve.wait_ge(own, p * OWN + 2 * PAIR_TILES + 2 + base)
                    dve.wait_ge(n_t, p * PAIR_TILES + 1)
                    for i in range(PAIR_TILES):
                        t = p * PAIR_TILES + i if isinstance(p, int) else dve.snap(p * PAIR_TILES + i)
                        dve.tensor_scalar(xn[:, i], feat[:, bass.ds(t, 1), :].rearrange("p o d -> p (o d)"),
                                          aggr[:, i, 0:1], rstd[:, i:i + 1], ALU.subtract, ALU.mult).then_inc(own, 1)
                    for i in range(PAIR_TILES):
                        t = p * PAIR_TILES + i if isinstance(p, int) else dve.snap(p * PAIR_TILES + i)
                        dve.wait_ge(own, p * OWN + 3 * PAIR_TILES + 2 + i + base)
                        dve.scalar_tensor_tensor(junk, xn[:, i], 1.0, wr_b[:], ALU.mult, ALU.mult,
                                                 accum_out=route[:, bass.ds(t, 1)]).then_inc(own, 1)
                    seven = feat[:, bass.ds(p * PAIR_TILES, PAIR_TILES), :]
                    dve.tensor_tensor(seven, seven, xn[:], ALU.add).then_inc(own, 1)
                    dve.wait_ge(own, p * OWN + OWN + base)
                    dve.sem_inc(a_passed, 1)

                onward = next_x if last else next_h
                scaled(0, 0)
                if last:
                    dve.wait_ge(x_in, 32)
                with dve.Fori(0, PAIRS - 1) as p:
                    scaled(dve.snap(p * 2 + 1), 1)
                    scaled(dve.snap(p * 2 + 2), 0)
                    onward(p)
                scaled(BLOCKS - 1, 1)
                onward(PAIRS - 1)

            @block.scalar
            def _(act):
                act.preload_act_table(ACT.Identity)
                act.sem_inc(a_out, HALVES)
                if last:
                    act.sem_inc(n_o, 1)
                if l == 0:
                    act.wait_ge(d_turned, 1)
                    act.activation(by_tile[:], hp[0][0:TILES, 0:P], ACT.Copy).then_inc(d_turned, 1)
                act.wait_ge(m_v, 6 if l == 0 else 5)
                if l == 0:
                    with act.Fori(0, PAIRS) as q:
                        for i in range(PAIR_TILES):
                            t = act.snap(q * PAIR_TILES + i)
                            act.activation(hh[:, 0, bass.ds(t * D, D)], h32[:, bass.ds(t * D, D)], ACT.Copy,
                                           scale=factor[:, bass.ds(t, 1)]).then_inc(m_hi, 1)
                else:
                    for i, t0 in enumerate(PIECES):
                        s = slice(t0 * D, (PIECES + (TILES,))[i + 1] * D)
                        act.activation(hh[:, 0, s], h32[:, s], ACT.Copy, scale=scale).then_inc(m_hi, 1)

                def out_block(b, par, pairs_done):
                    act.wait_ge(g_mm, pairs_done * PAIR_TILES + 1)
                    for f in range(HALVES):
                        act.wait_ge(a_scaled, b * HALVES + f + 1 + 2 * HALVES)
                        act.activation(fresh[:, f, par * BLK:(par + 1) * BLK], tmp[:, f],
                                       ACT.Identity if last else ACT.Relu, bias=gb_sb[:, l, f:f + 1],
                                       scale=unscale).then_inc(a_out, 1)

                def root_of(p):
                    act.wait_ge(own, p * OWN + 2 * PAIR_TILES + 1 + 1)
                    act.activation(rstd[:], rstd[:], ACT.Sqrt).then_inc(root, 1)
                    act.preload_act_table(ACT.Identity)

                def xn_out(p):
                    act.wait_ge(x_free, p + 1)
                    for i in range(PAIR_TILES):
                        act.wait_ge(n_t, p * PAIR_TILES + i + 2)
                        act.activation(xt[:, :, i * P:(i + 1) * P], xp[i % 2][:, 0:D].rearrange("p (f n) -> p f n", f=HALVES),
                                       ACT.Copy).then_inc(n_o, 1)

                out_block(0, 0, 0)
                start = 0
                if last:
                    out_block(1, 1, 0)
                    out_block(2, 0, 1)
                    root_of(0)
                    start = 1
                with act.Fori(start, PAIRS - 1) as p:
                    out_block(act.snap(p * 2 + 1), 1, p)
                    if last:
                        xn_out(act.snap(p - 1))
                    out_block(act.snap(p * 2 + 2), 0, p + 1)
                    if last:
                        root_of(p)
                out_block(BLOCKS - 1, 1, PAIRS - 1)
                if last:
                    xn_out(PAIRS - 2)
                    root_of(PAIRS - 1)
                    xn_out(PAIRS - 1)

            if l > 0:
                @block.gpsimd
                def _(pool):
                    pool.wait_ge(m_v, 1)
                    pool.partition_all_reduce(amax, pmax, P, RED.max).then_inc(m_p, 1)


def finish(nc, sem, nodes, big_a, big_b, ones, small, smalli, route, turned_xn, br_b, w1, b1_sb, w2, b2_b, out):
    with ExitStack() as ctx:
        def sb(name, shape, dt=F32):
            return ctx.enter_context(nc.sbuf_tensor(name, shape, dt))

        free = big_b[:].bitcast(F32)
        w1_sb = sb("w1_sb", [P, HALVES, HID])
        w2_sb = free[:, 0:HM * D].rearrange("p (m n) -> p m n", m=HM)
        hid = free[:, HM * D:HM * D + HM * PAIR_TILES * P].rearrange("p (m n) -> p m n", m=HM)
        xt = big_a[:].rearrange("p (c f n) -> p c f n", c=PAIRS, f=HALVES)
        summed = sb("summed", [P, 2, D])
        score, tie, col, ahead, chosen, gate, real, zeros, flags = (sb(n, [P, TILES]) for n in (
            "score", "tie", "col", "ahead", "chosen", "gate", "real", "zeros", "flags"))
        tri = sb("tri", [P, P])
        token = sb("token", [P, TILES], I32)
        part, greater, room = (small[:, i:i + 1] for i in (8, 9, 10))
        bound, tried, flip = (smalli[:, i:i + 1] for i in (1, 2, 3))
        psz = [ctx.enter_context(nc.psum_tensor(f"fp{i}", [P, 512], F32)) for i in range(8)]
        count = psz[6]
        counts = psz[7]
        steps = {"all": 0}
        w1_in, w2_in, x_in, s_c, s_v, s_part, s_count, s_m = (sem(n) for n in (
            "w1_in", "w2_in", "xt_in", "constants", "choice_step", "partial_count", "count_ready", "ties_ready"))
        h_mm, h_act, y_mm, y_out, o_dma, y_t, o_passed = (sem(n) for n in (
            "hidden_sum", "hidden_ready", "y_ready", "out_ready", "out_stored", "y_read", "o_passed"))
        with nc.Block() as block:
            @block.gpsimd
            def _(pool):
                pool.iota(token[:], pattern=[[P, TILES]], base=0, channel_multiplier=1).then_inc(s_c, 1)
                pool.memset(tri[:], 1.0).then_inc(s_c, 1)
                pool.wait_ge(s_c, 2)
                pool.affine_select(out=tri[:], in_=tri[:], compare_op=ALU.is_gt, fill=0.0, base=0,
                                   pattern=[[1, P]], channel_multiplier=-1).then_inc(s_c, 1)

            @block.sync
            def _(sp):
                sp.dma_start(w1_sb[:], w1.rearrange("(k p) n -> p k n", p=P)).then_inc(w1_in, 16)
                sp.dma_start(xt[:, 0].rearrange("p f n -> p (f n)"), turned_xn[0]).then_inc(x_in, 16)
                sp.dma_start(w2_sb, w2.rearrange("(m p) n -> p m n", p=P)).then_inc(w2_in, 16)
                for c in range(1, PAIRS):
                    sp.wait_ge(x_in, 16 * c)
                    sp.dma_start(xt[:, c].rearrange("p f n -> p (f n)"), turned_xn[c]).then_inc(x_in, 16)
                with sp.Fori(0, PAIRS - 1) as c:
                    sp.wait_ge(y_out, c * PAIR_TILES + PAIR_TILES)
                    sp.sem_inc(o_passed, 1)
                    sp.dma_start(out[bass.ds(c * PAIR_TILES * P, PAIR_TILES * P), :].rearrange("(t p) d -> p t d", p=P),
                                 nodes[:, bass.ds(c * PAIR_TILES, PAIR_TILES), :]).then_inc(o_dma, 16)
                sp.wait_ge(y_out, TILES - 1)
                sp.dma_start(out[(TILES - PAIR_TILES) * P:(TILES - 1) * P, :].rearrange("(t p) d -> p t d", p=P),
                             nodes[:, TILES - PAIR_TILES:TILES - 1, :]).then_inc(o_dma, 16)
                sp.wait_ge(y_out, TILES)
                sp.dma_start(out[(TILES - 1) * P:N, :], nodes[0:LAST, TILES - 1, :]).then_inc(o_dma, 16)
                sp.wait_ge(o_dma, (PAIRS + 1) * 16)

            @block.vector
            def _(dve):
                def done(ins, name=None):
                    steps["all"] += 1
                    if name:
                        steps[name] = steps["all"]
                    ins.then_inc(s_v, 1)
                    dve.wait_ge(s_v, steps["all"])

                dve.wait_ge(s_c, 3)
                done(dve.tensor_scalar(route[:], route[:], br_b[:], None, ALU.add))
                done(dve.tensor_scalar(real[:], token[:], float(N), None, ALU.is_lt))
                done(dve.tensor_scalar(zeros[:], real[:], -1.0, 3.4e38, ALU.add, ALU.mult))
                done(dve.tensor_tensor(score[:], route[:], real[:], ALU.mult))
                done(dve.tensor_tensor(score[:], score[:], zeros[:], ALU.add))
                done(dve.memset(zeros[:], 0.0))
                for r in range(32):
                    if r == 0:
                        ins = dve.tensor_scalar(flags[:], score[:], 0.0, 0.0, ALU.is_ge, ALU.add, accum_out=part)
                    else:
                        done(dve.tensor_scalar(tried, bound, 1 << (31 - r), None, ALU.bitwise_xor))
                        ins = dve.tensor_scalar(flags[:], score[:], tried.bitcast(F32), 0.0, ALU.is_ge, ALU.add,
                                                accum_out=part)
                    ins.then_inc(s_part, 1)
                    dve.wait_ge(s_count, r + 1)
                    if r == 0:
                        done(dve.tensor_scalar(bound, count[:, 0:1], float(KEEP), -1.0, ALU.is_ge, ALU.add))
                    else:
                        done(dve.tensor_scalar(flip, count[:, 0:1], float(KEEP), float(1 << (31 - r)), ALU.is_ge, ALU.mult))
                        done(dve.tensor_tensor(bound, bound, flip, ALU.bitwise_xor))
                edge = bound.bitcast(F32)
                done(dve.tensor_scalar(tie[:], score[:], edge, None, ALU.is_equal), "ties")
                dve.tensor_scalar(chosen[:], score[:], edge, 0.0, ALU.is_gt, ALU.add, accum_out=part).then_inc(s_part, 1)
                dve.wait_ge(s_part, 33)
                dve.wait_ge(s_m, 1)
                done(dve.tensor_scalar(room, counts[:, 128:129], -1.0, float(KEEP), ALU.mult, ALU.add))
                done(dve.tensor_copy(col[:], counts[:, 64:64 + TILES]))
                done(dve.tensor_tensor_scan(ahead[:], col[:], zeros[:], 0.0, ALU.add, ALU.add))
                done(dve.tensor_tensor(ahead[:], ahead[:], col[:], ALU.subtract))
                done(dve.tensor_tensor(ahead[:], ahead[:], counts[:, 0:TILES], ALU.add))
                done(dve.scalar_tensor_tensor(tie[:], ahead[:], room, tie[:], ALU.is_lt, ALU.mult))
                done(dve.tensor_tensor(chosen[:], chosen[:], tie[:], ALU.add))
                done(dve.tensor_tensor(gate[:], chosen[:], route[:], ALU.mult))

                with dve.Fori(0, PAIRS) as c:
                    for i in range(PAIR_TILES):
                        t = dve.snap(c * PAIR_TILES + i)
                        tile = nodes[:, bass.ds(t, 1), :].rearrange("p o d -> p (o d)")
                        dve.wait_ge(y_mm, t + 2)
                        dve.tensor_tensor(summed[:, i % 2], psz[4 + i % 2][:, 0:D], b2_b[:], ALU.add).then_inc(y_t, 1)
                        dve.wait_ge(y_t, t + 2)
                        dve.scalar_tensor_tensor(tile, summed[:, i % 2], gate[:, bass.ds(t, 1)], tile, ALU.mult,
                                                 ALU.add).then_inc(y_out, 1)
                        dve.wait_ge(y_out, t + 1)

            @block.tensor
            def _(pe):
                pe.sem_inc(h_act, 4)
                pe.sem_inc(y_mm, 1)
                pe.sem_inc(y_t, 1)

                def total(r):
                    pe.wait_ge(s_part, r + 1)
                    pe.matmul(count[:, 0:1], ones[:], part, start=True, stop=True).then_inc(s_count, 1)

                def hidden(c, m, counting):
                    for g in range(2):
                        r = (2 * m + g) % 4
                        pe.wait_ge(h_act, c * 2 * HM + 2 * m + g + 1)
                        for k in range(HALVES):
                            mm = pe.matmul(psz[r][:, 0:BLK], w1_sb[:, k, m * P:(m + 1) * P],
                                           xt[:, bass.ds(c, 1), k, g * BLK:(g + 1) * BLK].rearrange("p o n -> p (o n)"),
                                           start=k == 0, stop=k == HALVES - 1)
                            if k == HALVES - 1:
                                mm.then_inc(h_mm, 1)
                            if counting:
                                total(4 * m + 2 * g + k)

                def outputs(c):
                    pe.wait_ge(h_act, c * 2 * HM + 2 * HM + 4)
                    for i in range(PAIR_TILES):
                        t = c * PAIR_TILES + i if isinstance(c, int) else pe.snap(c * PAIR_TILES + i)
                        pe.wait_ge(y_t, t + 1 if i == 0 else t)
                        for m in range(HM):
                            mm = pe.matmul(psz[4 + i % 2][:, 0:D], hid[:, m, i * P:(i + 1) * P], w2_sb[:, m, :],
                                           start=m == 0, stop=m == HM - 1)
                        mm.then_inc(y_mm, 1)

                pe.wait_ge(w1_in, 16)
                pe.wait_ge(x_in, 16)
                for m in range(HM):
                    hidden(0, m, True)
                pe.wait_ge(s_part, 33)
                pe.wait_ge(s_v, steps["ties"])
                pe.matmul(counts[:, 0:TILES], tri[:], tie[:], start=True, stop=True)
                pe.matmul(counts[:, 128:129], ones[:], part, start=True, stop=True, skip_group_check=True)
                pe.matmul(counts[:, 64:64 + TILES], ones[:], tie[:], start=True, stop=True,
                          skip_group_check=True).then_inc(s_m, 1)
                pe.wait_ge(w2_in, 16)
                outputs(0)
                with pe.Fori(1, PAIRS) as c:
                    pe.wait_ge(x_in, c * 16 + 16)
                    for m in range(HM):
                        hidden(c, m, False)
                    outputs(c)

            @block.scalar
            def _(act):
                act.preload_act_table(ACT.Gelu_apprx_tanh)
                with act.Fori(0, PAIRS) as c:
                    for m in range(HM):
                        for g in range(2):
                            r = (2 * m + g) % 4
                            act.wait_ge(h_mm, c * 2 * HM + 2 * m + g + 1)
                            if m == 0 and g == 0:
                                act.wait_ge(y_mm, c * PAIR_TILES + 1)
                            act.activation(hid[:, m, g * BLK:(g + 1) * BLK], psz[r][:, 0:BLK], ACT.Gelu_apprx_tanh,
                                           bias=b1_sb[:, m:m + 1]).then_inc(h_act, 1)


_INS = ["x", "src", "dst", "L0_gnn_W1", "L0_gnn_b1", "L0_gnn_W2", "L0_gnn_b2", "L0_gnn_W3", "L0_gnn_b3",
        "L0_ffn_wr", "L0_ffn_br", "L0_ffn_w1", "L0_ffn_b1", "L0_ffn_w2", "L0_ffn_b2"]


def kernel(**inputs):
    import concourse.bacc as bacc
    from concourse.bass_utils import run_bass_kernel_spmd

    nc = bacc.Bacc("TRN2", target_bir_lowering=False, num_devices=1)
    arrays, a = {}, {}
    for name in _INS:
        array = np.ascontiguousarray(inputs[name])
        arrays[f"in_{name}"] = array
        a[name] = nc.dram_tensor(f"in_{name}", array.shape, mybir.dt.from_np(array.dtype), kind="ExternalInput").ap()
    out = nc.dram_tensor("out", (N, D), F32, kind="ExternalOutput").ap()
    build(nc, a["x"], a["src"], a["dst"], [a[f"L0_gnn_W{i}"] for i in (1, 2, 3)], [a[f"L0_gnn_b{i}"] for i in (1, 2, 3)],
          a["L0_ffn_wr"], a["L0_ffn_br"], a["L0_ffn_w1"], a["L0_ffn_b1"], a["L0_ffn_w2"], a["L0_ffn_b2"], out)
    r = run_bass_kernel_spmd(nc, [arrays], core_ids=[0])
    return r.results[0]["out"]
```
